# Optimizing a Trainium2 kernel written in Bass

```python
import numpy as np
import jax
import jax.numpy as jnp

def _softmax(x, axis=-1):
    return jax.nn.softmax(x, axis=axis)

def _gelu(x):
    return jax.nn.gelu(x, approximate=True)

def _silu(x):
    return jax.nn.silu(x)

def _sigmoid(x):
    return jax.nn.sigmoid(x)

def _layernorm(x, axis=-1, eps=1e-05):
    m = jnp.mean(x, axis=axis, keepdims=True)
    v = jnp.var(x, axis=axis, keepdims=True)
    return (x - m) / jnp.sqrt(v + eps)

def _scatter_add(tgt, idx, src, axis=0):
    return tgt.at[idx].add(src)

def _segment_sum(src, seg, n):
    return jax.ops.segment_sum(src, seg, n)
kernel_name = 'mk_xattn_ffn_d1_seqx_r8_a77561'

def setup_inputs(seed: int=0):
    np.random.seed(seed)
    _w = jnp.asarray

    def _rec_inputs():
        import jax
        import jax.numpy as jnp
        _rk = jax.random.key(seed)
        x = -0.0002928 + 1 * jax.random.normal(jax.random.fold_in(_rk, 1), (16, 128, 128), jnp.float32)
        _lenS = 128 - jax.random.randint(jax.random.fold_in(_rk, 7), (16,), 0, max(1, 128 // 4) + 1, jnp.int32)
        _lenS2 = 128 - jax.random.randint(jax.random.fold_in(_rk, 8), (16,), 0, max(1, 128 // 4) + 1, jnp.int32)
        _ctx_1024P = jax.random.normal(jax.random.fold_in(_rk, 11), (16, 16, 128), jnp.float32)
        _ctx_1024c = jax.random.dirichlet(jax.random.fold_in(_rk, 511), 0.3 * jnp.ones((16,), jnp.float32), (16, 128))
        _ctx_1024t = jnp.einsum('bsk,bkd->bsd', _ctx_1024c, _ctx_1024P)
        _ctx_1024t = _ctx_1024t * jax.lax.rsqrt(jnp.mean(jnp.square(_ctx_1024t)) + 1e-12) * 0.953939
        ctx_1024 = -1.39393e-06 + 0.999914 * (_ctx_1024t + 0.3 * jax.random.normal(jax.random.fold_in(_rk, 611), (16, 128, 128), jnp.float32))
        return (x, ctx_1024)
    x, ctx_1024 = _rec_inputs()

    def _L0_xattn_setup():
        import jax, jax.numpy as jnp
        import numpy as np
        B, S, D, NH = (2, 256, 128, 8)
        DH = D // NH
        EPS = 1e-06
        LN_EPS = 1e-05

        def _mlstm_cell(q, k, v, igate_w, igate_b, fgate_w, fgate_b, ln_scale):
            Slen = q.shape[0]
            ifg = jnp.concatenate([q, k, v], axis=-1)
            ig = (ifg @ igate_w.T + igate_b).T
            fg = (ifg @ fgate_w.T + fgate_b).T
            qh = q.reshape(Slen, NH, DH).transpose(1, 0, 2)
            kh = k.reshape(Slen, NH, DH).transpose(1, 0, 2)
            vh = v.reshape(Slen, NH, DH).transpose(1, 0, 2)
            log_f = jax.nn.log_sigmoid(fg)
            cs = jnp.cumsum(log_f, axis=1)
            fg_mat = cs[:, :, None] - cs[:, None, :]
            mask = jnp.tril(jnp.ones((Slen, Slen), dtype=bool))
            log_fg_mat = jnp.where(mask, fg_mat, -jnp.inf)
            log_D = log_fg_mat + ig[:, None, :]
            max_log_D = jnp.max(log_D, axis=-1, keepdims=True)
            D_mat = jnp.exp(log_D - max_log_D)
            qk = jnp.einsum('hsd,htd->hst', qh, kh) / np.sqrt(DH)
            C = qk * D_mat
            normalizer = jnp.maximum(jnp.abs(C.sum(axis=-1, keepdims=True)), jnp.exp(-max_log_D))
            h = jnp.einsum('hst,htd->hsd', C / (normalizer + EPS), vh)
            h = h.transpose(1, 0, 2).reshape(Slen, D)
            mu = h.mean(axis=-1, keepdims=True)
            var = h.var(axis=-1, keepdims=True)
            return (h - mu) / jnp.sqrt(var + LN_EPS) * ln_scale
        key = jax.random.key(seed)
        ks = jax.random.split(key, 8)
        rnd = lambda k, sh, s=1.0: jax.random.normal(k, sh, dtype=jnp.float32) * s
        return {'q': rnd(ks[0], (B, S, D)), 'k': rnd(ks[1], (B, S, D)), 'v': rnd(ks[2], (B, S, D)), 'igate_w': rnd(ks[3], (NH, 3 * D), 0.02), 'igate_b': jnp.linspace(3.0, 6.0, NH, dtype=jnp.float32), 'fgate_w': rnd(ks[4], (NH, 3 * D), 0.02), 'fgate_b': rnd(ks[5], (NH,), 0.3162278), 'ln_scale': jnp.ones((D,), dtype=jnp.float32)}
    _L0_xattn_all = _L0_xattn_setup()
    _L0_xattn_in = {k: v for k, v in _L0_xattn_all.items() if k in ('igate_w', 'igate_b', 'fgate_w', 'fgate_b', 'ln_scale')}
    del _L0_xattn_all

    def _L0_ffn_setup():
        import jax, jax.numpy as jnp
        import numpy as np
        import math
        D_IN = 128
        FEATURES = (512, 512, 128)
        BATCH, SEQ = (8, 256)

        def _conn_dense(kernel_bool, x):
            w = jnp.where(kernel_bool, jnp.float32(1.0), jnp.float32(-1.0))
            return x @ w
        key = jax.random.key(seed)
        kx, kk0, kk1, kk2 = jax.random.split(key, 4)
        x = jax.random.normal(kx, (BATCH, SEQ, D_IN), dtype=jnp.float32)
        k0 = jax.random.randint(kk0, (2 * D_IN, FEATURES[0]), 0, 2).astype(jnp.bool_)
        k1 = jax.random.randint(kk1, (FEATURES[0], FEATURES[1]), 0, 2).astype(jnp.bool_)
        k2 = jax.random.randint(kk2, (FEATURES[1], FEATURES[2]), 0, 2).astype(jnp.bool_)
        s0 = jnp.asarray(1.0 / math.sqrt(2 * D_IN), dtype=jnp.float32)
        s1 = jnp.asarray(1.0 / math.sqrt(FEATURES[0]), dtype=jnp.float32)
        s2 = jnp.asarray(1.0 / math.sqrt(FEATURES[1]), dtype=jnp.float32)
        return {'x': x, 'k0': k0, 'k1': k1, 'k2': k2, 's0': s0, 's1': s1, 's2': s2}
    _L0_ffn_all = _L0_ffn_setup()
    _L0_ffn_in = {k: v for k, v in _L0_ffn_all.items() if k in ('k0', 'k1', 'k2', 's0', 's1', 's2')}
    del _L0_ffn_all
    return {'x': x, 'ctx_1024': ctx_1024, 'L0_xattn_igate_w': _L0_xattn_in['igate_w'], 'L0_xattn_igate_b': _L0_xattn_in['igate_b'], 'L0_xattn_fgate_w': _L0_xattn_in['fgate_w'], 'L0_xattn_fgate_b': _L0_xattn_in['fgate_b'], 'L0_xattn_ln_scale': _L0_xattn_in['ln_scale'], 'L0_ffn_k0': _L0_ffn_in['k0'], 'L0_ffn_k1': _L0_ffn_in['k1'], 'L0_ffn_k2': _L0_ffn_in['k2'], 'L0_ffn_s0': _L0_ffn_in['s0'], 'L0_ffn_s1': _L0_ffn_in['s1'], 'L0_ffn_s2': _L0_ffn_in['s2']}

def reference(x, ctx_1024, L0_xattn_igate_w, L0_xattn_igate_b, L0_xattn_fgate_w, L0_xattn_fgate_b, L0_xattn_ln_scale, L0_ffn_k0, L0_ffn_k1, L0_ffn_k2, L0_ffn_s0, L0_ffn_s1, L0_ffn_s2):
    import jax
    import jax.numpy as jnp

    def _L0_xattn_ref(q, k, v, igate_w, igate_b, fgate_w, fgate_b, ln_scale):
        import jax, jax.numpy as jnp
        import numpy as np
        B, S, D, NH = (2, 256, 128, 8)
        DH = D // NH
        EPS = 1e-06
        LN_EPS = 1e-05

        def _mlstm_cell(q, k, v, igate_w, igate_b, fgate_w, fgate_b, ln_scale):
            Slen = q.shape[0]
            ifg = jnp.concatenate([q, k, v], axis=-1)
            ig = (ifg @ igate_w.T + igate_b).T
            fg = (ifg @ fgate_w.T + fgate_b).T
            qh = q.reshape(Slen, NH, DH).transpose(1, 0, 2)
            kh = k.reshape(Slen, NH, DH).transpose(1, 0, 2)
            vh = v.reshape(Slen, NH, DH).transpose(1, 0, 2)
            log_f = jax.nn.log_sigmoid(fg)
            cs = jnp.cumsum(log_f, axis=1)
            fg_mat = cs[:, :, None] - cs[:, None, :]
            mask = jnp.tril(jnp.ones((Slen, Slen), dtype=bool))
            log_fg_mat = jnp.where(mask, fg_mat, -jnp.inf)
            log_D = log_fg_mat + ig[:, None, :]
            max_log_D = jnp.max(log_D, axis=-1, keepdims=True)
            D_mat = jnp.exp(log_D - max_log_D)
            qk = jnp.einsum('hsd,htd->hst', qh, kh) / np.sqrt(DH)
            C = qk * D_mat
            normalizer = jnp.maximum(jnp.abs(C.sum(axis=-1, keepdims=True)), jnp.exp(-max_log_D))
            h = jnp.einsum('hst,htd->hsd', C / (normalizer + EPS), vh)
            h = h.transpose(1, 0, 2).reshape(Slen, D)
            mu = h.mean(axis=-1, keepdims=True)
            var = h.var(axis=-1, keepdims=True)
            return (h - mu) / jnp.sqrt(var + LN_EPS) * ln_scale
        return jax.vmap(lambda qq, kk, vv: _mlstm_cell(qq, kk, vv, igate_w, igate_b, fgate_w, fgate_b, ln_scale))(q, k, v)

    def _L0_ffn_ref(x, k0, k1, k2, s0, s1, s2):
        import jax, jax.numpy as jnp
        import numpy as np
        import math
        D_IN = 128
        FEATURES = (512, 512, 128)
        BATCH, SEQ = (8, 256)

        def _conn_dense(kernel_bool, x):
            w = jnp.where(kernel_bool, jnp.float32(1.0), jnp.float32(-1.0))
            return x @ w
        h = jnp.concatenate([x, -x], axis=-1)
        h = s0 * _conn_dense(k0, h)
        h = jax.nn.relu(h) * 2
        h = s1 * _conn_dense(k1, h)
        h = jax.nn.relu(h) * 2
        h = s2 * _conn_dense(k2, h)
        return h
    x = x + _L0_xattn_ref(_layernorm(x, axis=-1), ctx_1024, ctx_1024, L0_xattn_igate_w, L0_xattn_igate_b, L0_xattn_fgate_w, L0_xattn_fgate_b, L0_xattn_ln_scale)
    x = x + _L0_ffn_ref(_layernorm(x, axis=-1), L0_ffn_k0, L0_ffn_k1, L0_ffn_k2, L0_ffn_s0, L0_ffn_s1, L0_ffn_s2)
    return x

_drawn_inputs = setup_inputs


def setup_inputs(seed=0):
    import zlib

    import numpy as np

    out = dict(_drawn_inputs(seed))
    spreads = {'L0_xattn_ln_scale': (1.0, 0.2)}
    factors = {}
    for name, (base, spread) in spreads.items():
        noise = np.random.default_rng([zlib.crc32(name.encode()), seed]).standard_normal(out[name].shape)
        drawn = base * np.exp(spread * noise) if base else spread * noise
        out[name] = jnp.asarray(drawn.astype(out[name].dtype))
    for name, factor in factors.items():
        out[name] = (out[name] * factor).astype(out[name].dtype)
    return out
```

```python
from contextlib import ExitStack

import concourse.bass as bass
from concourse import mybir

F32 = mybir.dt.float32
F16 = mybir.dt.float16
U8 = mybir.dt.uint8
ALU = mybir.AluOpType
ACT = mybir.ActivationFunctionType

B, S, D = 16, 128, 128
NH = 8
DH = D // NH
GB = 4
NG = B // GB
F = 512
FT = F // 128
VW = 32
ONE = DH
TOK = GB * S
LN_EPS = 1e-5
EPS = 1e-6
NEVER = 1e30
QK_SCALE = 1.0 / DH ** 0.5
X2_SCALE = 2.0 ** 12
W0_SCALE = 2.0 ** -4
W1_SCALE = 2.0 ** -9
OUT_SCALE = 8.0 / (X2_SCALE * W0_SCALE * W1_SCALE)


def place(h):
    return 4 * (h // 2 % 2) + 2 * (h // 4) + h % 2


def xattn_ffn(nc, x, ctx_in, igate_w, igate_b, fgate_w, fgate_b, ln_scale, k0, k1, k2, s0, s1, s2, running_max, out):
    with ExitStack() as stack:
        def sb(name, shape, dt=F32):
            return stack.enter_context(nc.sbuf_tensor(name, shape, dt))

        def ps(name, shape, dt=F32):
            return stack.enter_context(nc.psum_tensor(name, shape, dt))

        def sem(name):
            return stack.enter_context(nc.semaphore(name))

        ident = sb("ident", [128, 128])
        ident16 = sb("ident16", [128, 128], F16)
        odd_heads = sb("odd_heads", [128, 1])
        gate_rows = sb("gate_rows", [2 * NH, 3 * D])
        wq = sb("wq", [128, 2, VW])
        wkv = sb("wkv", [128, 2, VW])
        gate_b = sb("gate_b", [128, 2])
        lns = sb("lns", [128, D])
        minus_half = sb("minus_half", [128, GB])
        s_in = sb("s_in", [128, 3])
        s_work = sb("s_work", [128, 8])
        k0_in = sb("k0_in", [128, 2, F], U8)
        k1_in = sb("k1_in", [128, FT, F], U8)
        k2_in = sb("k2_in", [128, FT, D], U8)
        w0 = sb("w0", [128, F], F16)
        w1 = sb("w1", [128, FT, F], F16)
        w2 = sb("w2", [128, FT, D], F16)
        xs = sb("xs", [128, 2, GB, D])
        cs_in = sb("cs_in", [128, 2, GB, D])
        vals = sb("vals", [128, 2, GB, NH, VW])
        xn = sb("xn", [128, GB, D])
        st_q = sb("st_q", [128, GB, 6])
        mv_q = sb("mv_q", [128, GB, 2])
        rs_q = sb("rs_q", [128, GB])
        ve_q = sb("ve_q", [128, GB])
        qkT = sb("qkT", [128, 2, GB, 3, S])
        f_min = sb("f_min", [128, S])
        f_abs = sb("f_abs", [128, S])
        f_exp = sb("f_exp", [128, S])
        f_ln = sb("f_ln", [128, S])
        cumf = sb("cumf", [128, S])
        a_row = sb("a_row", [128, S])
        max_row = sb("max_row", [128, 2, S])
        m_row = sb("m_row", [128, S])
        aT = sb("aT", [128, 2, GB, VW])
        em = sb("em", [128, 2, GB, VW])
        maxb = sb("maxb", [128, 2, GB, NH, S])
        dmat = sb("dmat", [128, 2, NH, S])
        cmat = sb("cmat", [128, 2, NH, S])
        oT = sb("oT", [128, 2, 2, S])
        den = sb("den", [128, 2, NH])
        hatt = sb("hatt", [128, 2, D])
        st_h = sb("st_h", [128, 2, 6])
        mv_h = sb("mv_h", [128, 2, 2])
        ve_h = sb("ve_h", [128, 2])
        rs_h = sb("rs_h", [128, 2])
        hsc = sb("hsc", [128, 2, D])
        x1 = sb("x1", [128, 3, GB, D])
        st_x = sb("st_x", [128, 2, 6])
        mv_x = sb("mv_x", [128, 2, 2])
        ve_x = sb("ve_x", [128, 2])
        rs_x = sb("rs_x", [128, 2])
        x2 = sb("x2", [128, 2, D])
        x2p = sb("x2p", [128, 2, 2, D], F16)
        x2T = sb("x2T", [128, 2, TOK], F16)
        h1 = sb("h1", [128, FT, 2, TOK], F16)
        h2 = sb("h2", [128, FT, 2, TOK], F16)
        outb = sb("outb", [128, 2, GB, D])
        pT = ps("pT", [128, 2, 2, S])
        pG = ps("pG", [128, 4, S])
        pS = ps("pS", [128, NH, S])
        pO = ps("pO", [128, 4, S])
        pX = ps("pX", [128, 2, TOK], F16)
        pF = [ps(f"pF{i}", [128, TOK], F32) for i in range(2)]

        ctx_loaded = [sem(f"ctx_loaded{p}") for p in range(2)]
        x_loaded = [sem(f"x_loaded{p}") for p in range(2)]
        gatew_loaded = sem("gatew_loaded")
        gateb_loaded = sem("gateb_loaded")
        ffnw_loaded = sem("ffnw_loaded")
        consts_ready = sem("consts_ready")
        cleared = sem("cleared")
        gatew_turned = sem("gatew_turned")
        gatew_ready = sem("gatew_ready")
        ffnw_ready = sem("ffnw_ready")
        q_stats = sem("q_stats")
        q_rstd = sem("q_rstd")
        xn_ready = sem("xn_ready")
        vals_ready = sem("vals_ready")
        turned = sem("turned")
        turned_out = sem("turned_out")
        gates_ready = sem("gates_ready")
        f_min_ready = sem("f_min_ready")
        f_ln_ready = sem("f_ln_ready")
        max_ready = sem("max_ready")
        m_ready = sem("m_ready")
        am_turned = sem("am_turned")
        am_ready = sem("am_ready")
        max_stored = sem("max_stored")
        max_spread = [[sem(f"max_spread{p}{j}") for j in range(GB)] for p in range(2)]
        bank_written = sem("bank_written")
        exp_ready = sem("exp_ready")
        masked = sem("masked")
        c_ready = sem("c_ready")
        pv_ready = sem("pv_ready")
        oT_ready = sem("oT_ready")
        o_turned = sem("o_turned")
        o_read = sem("o_read")
        h_stats = sem("h_stats")
        h_rstd = sem("h_rstd")
        x_stats = sem("x_stats")
        x_rstd = sem("x_rstd")
        x1_ready = sem("x1_ready")
        x2_ready = sem("x2_ready")
        x2_high = sem("x2_high")
        x2_low = sem("x2_low")
        x2_turned = sem("x2_turned")
        x2T_ready = sem("x2T_ready")
        ffn_sums = sem("ffn_sums")
        ffn_high = sem("ffn_high")
        ffn_low = sem("ffn_low")
        out_ready = sem("out_ready")
        out_stored = [sem(f"out_stored{p}") for p in range(2)]
        dve_own = sem("dve_own")
        act_own = sem("act_own")
        pool_own = sem("pool_own")

        def group_rows(dram, g):
            return dram[GB * g:GB * (g + 1)].rearrange("b s d -> s b d")

        def load(sp, g):
            if g >= 2:
                sp.wait_ge(am_turned, g - 1)
                sp.wait_ge(vals_ready, g - 1)
                sp.wait_ge(x1_ready, GB * (g - 1))
            sp.dma_start(xs[:, g % 2], group_rows(x, g)).then_inc(x_loaded[g % 2], 16)
            sp.dma_start(cs_in[:, g % 2], group_rows(ctx_in, g)).then_inc(ctx_loaded[g % 2], 16)

        def store(sp, g):
            sp.wait_ge(out_ready, g + 1)
            sp.dma_start(group_rows(out, g), outb[:, g % 2]).then_inc(out_stored[g % 2], 16)

        block = stack.enter_context(nc.Block())

        @block.sync
        def _(sp):
            sp.dma_start(cs_in[:, 0], group_rows(ctx_in, 0)).then_inc(ctx_loaded[0], 16)
            sp.dma_start(gate_rows[0:NH, :], igate_w).then_inc(gatew_loaded, 16)
            sp.dma_start(gate_rows[NH:2 * NH, :], fgate_w).then_inc(gatew_loaded, 16)
            sp.wait_ge(cleared, 1)
            for j in range(GB):
                for n, bias in enumerate((igate_b, fgate_b)):
                    sp.dma_start(gate_b[32 * j:32 * j + NH, n:n + 1], bias.rearrange("(h a) -> h a", a=1)).then_inc(gateb_loaded, 16)
            sp.dma_start(lns[:, :], ln_scale.rearrange("(a d) -> a d", a=1).broadcast_to([128, D])).then_inc(ffnw_loaded, 16)
            for n, s in enumerate((s0, s1, s2)):
                sp.dma_start(s_in[:, n:n + 1], s.rearrange("(a d) -> a d", a=1).broadcast_to([128, 1])).then_inc(ffnw_loaded, 16)
            sp.dma_start(k0_in[:, :, :], k0.rearrange("(c p) n -> p c n", p=128)).then_inc(ffnw_loaded, 16)
            sp.dma_start(k1_in[:, :, :], k1.rearrange("(c p) n -> p c n", p=128)).then_inc(ffnw_loaded, 16)
            sp.dma_start(k2_in[:, :, :], k2.rearrange("(c p) n -> p c n", p=128)).then_inc(ffnw_loaded, 16)
            load(sp, 1)
            for g in range(NG):
                p = g % 2
                sp.wait_ge(max_ready, g + 1)
                for j in range(GB):
                    sp.dma_start(running_max[g, j], max_row[32 * j:32 * j + NH, p, :]).then_inc(max_stored, 16)
                sp.wait_ge(max_stored, 16 * GB * (g + 1))
                if g >= 2:
                    sp.wait_ge(exp_ready, GB * (g - 1))
                for j in range(GB):
                    sp.dma_start(maxb[:, p, j], running_max[g:g + 1, j].broadcast_to([128, NH, S])).then_inc(max_spread[p][j], 16)
                if 1 <= g < NG - 1:
                    load(sp, g + 1)
                if g >= 2:
                    store(sp, g - 2)
            store(sp, NG - 2)
            store(sp, NG - 1)
            for p in range(2):
                sp.wait_ge(out_stored[p], 16 * (NG // 2))

        @block.tensor
        def _(pe):
            def turn(g, j):
                n = GB * g + j
                if j == 0:
                    pe.wait_ge(ctx_loaded[g % 2], 16 * (g // 2 + 1))
                pe.wait_ge(xn_ready, n + 1)
                if n >= 1:
                    pe.wait_ge(turned_out, n)
                pe.transpose(pT[:, 0, 0], xn[:, j], ident[:, :])
                pe.transpose(pT[:, 0, 1], cs_in[:, g % 2, j], ident[:, :]).then_inc(turned, 1)

            def gates(g):
                if g == 0:
                    pe.wait_ge(gatew_ready, 1)
                else:
                    pe.wait_ge(am_ready, g)
                pe.wait_ge(turned_out, GB * (g + 1))
                for n in range(2):
                    for part, w in enumerate((wq, wkv)):
                        for j in range(GB):
                            last = pe.matmul(pG[32 * j:32 * j + VW, n], w[:, n, :], qkT[:, g % 2, j, part],
                                             start=(part == 0), stop=(part == 1))
                last.then_inc(gates_ready, 1)

            def turn_am(g):
                pe.wait_ge(m_ready, g + 1)
                pe.transpose(pG[:, 2], a_row[:, :], ident[:, :])
                pe.transpose(pG[:, 3], m_row[:, :], ident[:, :]).then_inc(am_turned, 1)

            def scores(g, j):
                n = GB * g + j
                if n >= 1:
                    pe.wait_ge(c_ready, n)
                q, c, q_odd = (qkT[:, g % 2, j, i] for i in range(3))
                for i in range(NH // 2):
                    r = 32 * i
                    if i >= 2:
                        pe.wait_ge(bank_written, 4 * n + i - 1)
                    pe.matmul(pS[:, place(2 * i)], c[r:r + DH], q[r:r + DH], start=True, stop=True)
                    pe.matmul(pS[:, place(2 * i + 1)], c[r:r + 32], q_odd[r:r + 32], start=True, stop=True).then_inc(bank_written, 1)

            def weigh(g, j):
                n = GB * g + j
                if j == 0:
                    pe.wait_ge(vals_ready, g + 1)
                pe.wait_ge(c_ready, n + 1)
                if n >= 1:
                    pe.wait_ge(o_read, n)
                for half in range(2):
                    for i in range(4):
                        h = 4 * half + i
                        last = pe.matmul(pO[32 * i:32 * i + VW, half], vals[:, g % 2, j, h], cmat[:, n % 2, place(h)],
                                         start=True, stop=True)
                last.then_inc(pv_ready, 1)

            def turn_o(g, j):
                n = GB * g + j
                pe.wait_ge(oT_ready, n + 1)
                for half in range(2):
                    last = pe.transpose(pO[:, 2 + half], oT[:, n % 2, half], ident[:, :])
                last.then_inc(o_turned, 1)

            def turn_x2(g, j):
                n = GB * g + j
                if j == 0 and g >= 1:
                    pe.wait_ge(x2T_ready, g)
                pe.wait_ge(x2_high, n + 1)
                pe.wait_ge(x2_low, n + 1)
                for part in range(2):
                    last = pe.transpose(pX[:, part, S * j:S * (j + 1)], x2p[:, n % 2, part], ident16[:, :])
                last.then_inc(x2_turned, 1)

            def bank_free(g, m):
                if m >= 2:
                    pe.wait_ge(ffn_low, 2 * FT * g + m - 1)
                elif g >= 1 and m == 0:
                    pe.wait_ge(out_ready, g)
                elif g >= 1:
                    pe.wait_ge(ffn_low, 2 * FT * g)

            def ffn0(g, m):
                if m == 0:
                    pe.wait_ge(ffnw_ready, 1)
                    pe.wait_ge(x2T_ready, g + 1)
                bank_free(g, m)
                for part in range(2):
                    last = pe.matmul(pF[m % 2][:, :], w0[:, 128 * m:128 * (m + 1)], x2T[:, part],
                                     start=(part == 0), stop=(part == 1))
                last.then_inc(ffn_sums, 1)

            def ffn1(g, m):
                bank_free(g, FT + m)
                for k in range(FT):
                    pe.wait_ge(ffn_low, 2 * FT * g + k + 1)
                    for part in range(2):
                        last = pe.matmul(pF[m % 2][:, :], w1[:, k, 128 * m:128 * (m + 1)], h1[:, k, part],
                                         start=(k == 0 and part == 0), stop=(k == FT - 1 and part == 1))
                last.then_inc(ffn_sums, 1)

            def ffn2(g):
                pe.wait_ge(ffn_low, 2 * FT * (g + 1))
                for j in range(GB):
                    for k in range(FT):
                        for part in range(2):
                            last = pe.matmul(pF[0][:, D * j:D * (j + 1)], h2[:, k, part, S * j:S * (j + 1)], w2[:, k],
                                             start=(k == 0 and part == 0), stop=(k == FT - 1 and part == 1))
                last.then_inc(ffn_sums, 1)

            pe.wait_ge(consts_ready, 1)
            pe.wait_ge(gatew_loaded, 32)
            for part in range(3):
                last = pe.transpose(pG[:, part, 0:2 * NH], gate_rows[:, D * part:D * (part + 1)], ident[0:2 * NH, 0:2 * NH])
            last.then_inc(gatew_turned, 1)
            for j in range(GB):
                turn(0, j)
            gates(0)
            turn_am(0)
            for g in range(NG):
                f = g - 1
                scores(g, 0)
                if f >= 0:
                    turn_x2(f, GB - 1)
                if f >= 1:
                    ffn2(f - 1)
                if g + 1 < NG:
                    turn(g + 1, 0)
                    turn(g + 1, 1)
                weigh(g, 0)
                scores(g, 1)
                if f >= 0:
                    ffn0(f, 0)
                    ffn0(f, 1)
                turn_o(g, 0)
                if f >= 0:
                    ffn0(f, 2)
                if g + 1 < NG:
                    turn(g + 1, 2)
                    turn(g + 1, 3)
                weigh(g, 1)
                if f >= 0:
                    ffn0(f, 3)
                if g + 1 < NG:
                    gates(g + 1)
                scores(g, 2)
                if f >= 0:
                    ffn1(f, 0)
                turn_o(g, 1)
                turn_x2(g, 0)
                if f >= 0:
                    ffn1(f, 1)
                weigh(g, 2)
                if g + 1 < NG:
                    turn_am(g + 1)
                scores(g, 3)
                if f >= 0:
                    ffn1(f, 2)
                turn_o(g, 2)
                turn_x2(g, 1)
                if f >= 0:
                    ffn1(f, 3)
                weigh(g, 3)
                turn_x2(g, 2)
                turn_o(g, 3)
            f = NG - 1
            turn_x2(f, GB - 1)
            ffn2(f - 1)
            for m in range(FT):
                ffn0(f, m)
            for m in range(FT):
                ffn1(f, m)
            ffn2(f)

        @block.scalar
        def _(act):
            own = [0]

            def step(ins):
                own[0] += 1
                ins.then_inc(act_own, 1)
                act.wait_ge(act_own, own[0])

            def turn_out(g, j):
                n = GB * g + j
                act.wait_ge(turned, n + 1)
                if j == 0 and g >= 2:
                    act.wait_ge(bank_written, 4 * GB * (g - 1))
                act.copy(qkT[:, g % 2, j, 0:2], pT[:, 0])
                act.activation(qkT[:, g % 2, j, 2], pT[:, 0, 0], ACT.Copy, scale=odd_heads[:, 0:1]).then_inc(turned_out, 1)

            def gate_logs(g):
                act.wait_ge(f_min_ready, g + 1)
                step(act.activation(f_abs[:, :], pG[:, 1], ACT.Abs, bias=gate_b[:, 1:2]))
                step(act.activation(f_exp[:, :], f_abs[:, :], ACT.Exp, scale=-1.0))
                act.activation(f_ln[:, :], f_exp[:, :], ACT.Ln, bias=1.0).then_inc(f_ln_ready, 1)

            def gate_out(g):
                act.wait_ge(am_turned, g + 1)
                if g >= 2:
                    act.wait_ge(o_read, GB * (g - 1))
                act.copy(aT[:, g % 2].rearrange("p j h -> p (j h)"), pG[:, 2])
                e = em[:, g % 2].rearrange("p j h -> p (j h)")
                step(act.activation(e, pG[:, 3], ACT.Exp, scale=-1.0))
                act.activation(e, e, ACT.Copy, bias=EPS).then_inc(am_ready, 1)

            def decay(g, j, heads):
                n = GB * g + j
                if heads[0] == 0:
                    act.wait_ge(am_ready, g + 1)
                    act.wait_ge(masked, n + 1)
                    if n >= 2:
                        act.wait_ge(c_ready, n - 1)
                for h in heads:
                    last = act.activation(dmat[:, n % 2, place(h)], maxb[:, g % 2, j, h], ACT.Exp,
                                          bias=aT[:, g % 2, j, h:h + 1], scale=-1.0)
                if heads[-1] == NH - 1:
                    last.then_inc(exp_ready, 1)

            def take_o(g, j):
                n = GB * g + j
                act.wait_ge(pv_ready, n + 1)
                if n >= 2:
                    act.wait_ge(o_turned, n - 1)
                act.copy(oT[:, n % 2], pO[:, 0:2]).then_inc(oT_ready, 1)

            def x2_take_high(g, j):
                n = GB * g + j
                act.wait_ge(x2_ready, n + 1)
                if n >= 2:
                    act.wait_ge(x2_turned, n - 1)
                act.copy(x2p[:, n % 2, 0], x2[:, n % 2]).then_inc(x2_high, 1)

            def high(g, m):
                act.wait_ge(ffn_sums, (2 * FT + 1) * g + m + 1)
                dst = h1 if m < FT else h2
                if m == 0 and g >= 1:
                    act.wait_ge(ffn_sums, (2 * FT + 1) * g)
                act.activation(dst[:, m % FT, 0], pF[m % 2][:, :], ACT.Relu).then_inc(ffn_high, 1)

            act.dma_start(xs[:, 0], group_rows(x, 0)).then_inc(x_loaded[0], 16)
            act.wait_ge(consts_ready, 1)
            for j in range(GB):
                turn_out(0, j)
            act.wait_ge(gateb_loaded, 16 * 2 * GB)
            gate_logs(0)
            gate_out(0)
            decay(0, 0, range(NH))
            lo, hi = range(NH // 2), range(NH // 2, NH)
            for g in range(NG):
                f = g - 1
                nxt = g + 1 < NG
                if f >= 0:
                    x2_take_high(f, GB - 1)
                decay(g, 1, lo)
                if nxt:
                    turn_out(g + 1, 0)
                    turn_out(g + 1, 1)
                decay(g, 1, hi)
                take_o(g, 0)
                if f >= 0:
                    high(f, 0)
                    high(f, 1)
                decay(g, 2, lo)
                if f >= 0:
                    high(f, 2)
                if nxt:
                    turn_out(g + 1, 2)
                    turn_out(g + 1, 3)
                decay(g, 2, hi)
                if f >= 0:
                    high(f, 3)
                take_o(g, 1)
                x2_take_high(g, 0)
                if nxt:
                    gate_logs(g + 1)
                decay(g, 3, lo)
                if f >= 0:
                    high(f, 4)
                decay(g, 3, hi)
                take_o(g, 2)
                if f >= 0:
                    high(f, 5)
                x2_take_high(g, 1)
                if nxt:
                    gate_out(g + 1)
                if f >= 0:
                    high(f, 6)
                if nxt:
                    decay(g + 1, 0, range(NH))
                take_o(g, 3)
                if f >= 0:
                    high(f, 7)
                x2_take_high(g, 2)
            f = NG - 1
            x2_take_high(f, GB - 1)
            for m in range(2 * FT):
                high(f, m)

        @block.vector
        def _(dve):
            own = [0]

            def mark(ins):
                own[0] += 1
                ins.then_inc(dve_own, 1)
                return own[0]

            def step(ins):
                dve.wait_ge(dve_own, mark(ins))

            def norm_q_stats(g):
                p = g % 2
                dve.wait_ge(x_loaded[p], 16 * (g // 2 + 1))
                for j in range(GB):
                    last = mark(dve.bn_stats(st_q[:, j], xs[:, p, j]))
                for j in range(GB):
                    dve.wait_ge(dve_own, last - GB + 1 + j)
                    agg = dve.bn_aggr(mv_q[:, j], st_q[:, j])
                agg.then_inc(q_stats, 1)

            def norm_q(g):
                dve.wait_ge(q_rstd, g + 1)
                dve.wait_ge(q_stats, g + 1)
                if g >= 1:
                    dve.wait_ge(turned, GB * g)
                for j in range(GB):
                    dve.tensor_scalar(xn[:, j], xs[:, g % 2, j], mv_q[:, j, 0:1], rs_q[:, j:j + 1],
                                      ALU.subtract, ALU.mult).then_inc(xn_ready, 1)

            def forget_min(g):
                dve.wait_ge(gates_ready, g + 1)
                if g == 0:
                    dve.wait_ge(gateb_loaded, 16 * 2 * GB)
                dve.tensor_scalar(f_min[:, :], pG[:, 1], gate_b[:, 1:2], 0.0, ALU.add, ALU.min).then_inc(f_min_ready, 1)

            def gate_scans(g):
                dve.wait_ge(f_ln_ready, g + 1)
                dve.wait_ge(f_min_ready, g + 1)
                step(dve.tensor_tensor_scan(cumf[:, :], f_min[:, :], f_ln[:, :], 0.0, ALU.add, ALU.subtract))
                if g >= 1:
                    dve.wait_ge(am_turned, g)
                step(dve.scalar_tensor_tensor(out=a_row[:, :], in0=pG[:, 0], scalar=gate_b[:, 0:1], in1=cumf[:, :],
                                              op0=ALU.add, op1=ALU.subtract))
                if g >= 2:
                    dve.wait_ge(max_stored, 16 * GB * (g - 1))
                dve.tensor_tensor_scan(max_row[:, g % 2], a_row[:, :], a_row[:, :], -3.0e38, ALU.max, ALU.max).then_inc(max_ready, 1)
                dve.wait_ge(max_ready, g + 1)
                dve.tensor_tensor(m_row[:, :], cumf[:, :], max_row[:, g % 2], ALU.add).then_inc(m_ready, 1)

            def make_c(g, j):
                n = GB * g + j
                dve.wait_ge(bank_written, 4 * (n + 1))
                dve.wait_ge(exp_ready, n + 1)
                if n >= 2:
                    dve.wait_ge(pv_ready, n - 1)
                dve.scalar_tensor_tensor(out=cmat[:, n % 2].rearrange("p h s -> p (h s)"),
                                         in0=pS[:, :].rearrange("p h s -> p (h s)"), scalar=QK_SCALE,
                                         in1=dmat[:, n % 2].rearrange("p h s -> p (h s)"),
                                         op0=ALU.mult, op1=ALU.mult).then_inc(c_ready, 1)

            def head_out(g, j):
                n = GB * g + j
                e = n % 2
                o = pO[:, 2:4].rearrange("p a (i v) -> p (a i) v", v=VW)
                dve.wait_ge(o_turned, n + 1)
                dve.wait_ge(am_ready, g + 1)
                step(dve.scalar_tensor_tensor(out=den[:, e], in0=o[:, :, ONE], scalar=EPS, in1=em[:, g % 2, j, 0:NH],
                                              op0=ALU.subtract, op1=ALU.max, reverse0=True))
                step(dve.scalar_tensor_tensor(out=den[:, e], in0=o[:, :, ONE], scalar=EPS, in1=den[:, e],
                                              op0=ALU.add, op1=ALU.max))
                step(dve.reciprocal(den[:, e], den[:, e]))
                dve.tensor_tensor(hatt[:, e].rearrange("p (h d) -> p h d", d=DH), o[:, :, 0:DH],
                                  den[:, e].unsqueeze(2).broadcast_to([128, NH, DH]), ALU.mult).then_inc(o_read, 1)
                dve.wait_ge(o_read, n + 1)
                step(dve.bn_stats(st_h[:, e], hatt[:, e]))
                dve.bn_aggr(mv_h[:, e], st_h[:, e]).then_inc(h_stats, 1)
                dve.wait_ge(h_stats, n + 1)
                mark(dve.scalar_tensor_tensor(out=hsc[:, e], in0=hatt[:, e], scalar=mv_h[:, e, 0:1], in1=lns[:, :],
                                              op0=ALU.subtract, op1=ALU.mult))
                return own[0]

            def residual(g, j, scaled):
                n = GB * g + j
                e = n % 2
                if j == 0 and g >= 3:
                    dve.wait_ge(out_ready, g - 2)
                dve.wait_ge(dve_own, scaled)
                dve.wait_ge(h_rstd, n + 1)
                dve.scalar_tensor_tensor(out=x1[:, g % 3, j], in0=hsc[:, e], scalar=rs_h[:, e:e + 1], in1=xs[:, g % 2, j],
                                         op0=ALU.mult, op1=ALU.add).then_inc(x1_ready, 1)
                dve.wait_ge(x1_ready, n + 1)
                step(dve.bn_stats(st_x[:, e], x1[:, g % 3, j]))
                dve.bn_aggr(mv_x[:, e], st_x[:, e]).then_inc(x_stats, 1)

            def norm_x(g, j):
                n = GB * g + j
                e = n % 2
                dve.wait_ge(x_rstd, n + 1)
                dve.wait_ge(x_stats, n + 1)
                if n >= 2:
                    dve.wait_ge(x2_high, n - 1)
                    dve.wait_ge(x2_low, n - 1)
                dve.tensor_scalar(x2[:, e], x1[:, g % 3, j], mv_x[:, e, 0:1], rs_x[:, e:e + 1],
                                  ALU.subtract, ALU.mult).then_inc(x2_ready, 1)

            def take_x2T(g):
                dve.wait_ge(x2_turned, GB * (g + 1))
                if g >= 1:
                    dve.wait_ge(ffn_sums, (2 * FT + 1) * (g - 1) + FT)
                dve.tensor_copy(x2T[:, :, :], pX[:, :, :]).then_inc(x2T_ready, 1)

            def low(g, m):
                dve.wait_ge(ffn_high, 2 * FT * g + m + 1)
                dst = h1 if m < FT else h2
                dve.scalar_tensor_tensor(out=dst[:, m % FT, 1], in0=pF[m % 2][:, :], scalar=0.0, in1=dst[:, m % FT, 0],
                                         op0=ALU.max, op1=ALU.subtract).then_inc(ffn_low, 1)

            def finish(g):
                dve.wait_ge(ffn_sums, (2 * FT + 1) * (g + 1))
                if g >= 2:
                    dve.wait_ge(out_stored[g % 2], 16 * (g // 2))
                dve.scalar_tensor_tensor(out=outb[:, g % 2].rearrange("p j d -> p (j d)"), in0=pF[0][:, :],
                                         scalar=s_work[:, 7:8], in1=x1[:, g % 3].rearrange("p j d -> p (j d)"),
                                         op0=ALU.mult, op1=ALU.add).then_inc(out_ready, 1)

            def ffn_weights():
                dve.wait_ge(ffnw_loaded, 16 * 7)
                step(dve.tensor_scalar(s_work[:, 0:2], s_in[:, 0:2], 0.0, 2.0, ALU.is_ge, ALU.mult))
                step(dve.tensor_scalar(s_work[:, 0:2], s_work[:, 0:2], 1.0, None, ALU.subtract))
                step(dve.tensor_tensor(s_work[:, 2:4], s_work[:, 0:2], s_in[:, 0:2], ALU.mult))
                step(dve.tensor_scalar(s_work[:, 4:5], s_work[:, 0:1], W0_SCALE, None, ALU.mult))
                step(dve.tensor_scalar(s_work[:, 5:6], s_work[:, 1:2], 2.0 * W1_SCALE, None, ALU.mult))
                step(dve.tensor_scalar(s_work[:, 6:7], s_work[:, 1:2], W1_SCALE, None, ALU.mult))
                step(dve.tensor_tensor(s_work[:, 7:8], s_work[:, 2:3], s_work[:, 3:4], ALU.mult))
                step(dve.tensor_tensor(s_work[:, 7:8], s_work[:, 7:8], s_in[:, 2:3], ALU.mult))
                step(dve.tensor_scalar(s_work[:, 7:8], s_work[:, 7:8], OUT_SCALE, None, ALU.mult))
                step(dve.tensor_tensor(w0[:, :], k0_in[:, 0], k0_in[:, 1], ALU.subtract))
                step(dve.tensor_scalar(w0[:, :], w0[:, :], s_work[:, 4:5], None, ALU.mult))
                step(dve.tensor_scalar(w1[:, :, :], k1_in[:, :, :], s_work[:, 5:6], s_work[:, 6:7], ALU.mult, ALU.subtract))
                dve.tensor_scalar(w2[:, :, :], k2_in[:, :, :], 2.0, 1.0, ALU.mult, ALU.subtract).then_inc(ffnw_ready, 1)

            step(dve.memset(gate_b[:, :], 0.0))
            step(dve.memset(wq[:, :, :], 0.0))
            dve.memset(wkv[:, :, :], 0.0).then_inc(cleared, 1)
            dve.wait_ge(cleared, 1)
            norm_q_stats(0)
            norm_q(0)
            dve.wait_ge(gatew_turned, 1)
            def gate_cols(part):
                return pG[:, part, 0:2 * NH].rearrange("p (n h) -> p n h", n=2)
            step(dve.tensor_copy(wq[:, :, 0:NH], gate_cols(0)))
            step(dve.tensor_copy(wkv[:, :, 0:NH], gate_cols(1)))
            dve.tensor_tensor(wkv[:, :, 0:NH], gate_cols(2), wkv[:, :, 0:NH], ALU.add).then_inc(gatew_ready, 1)
            forget_min(0)
            gate_scans(0)
            ffn_weights()
            for g in range(NG):
                f = g - 1
                nxt = g + 1 < NG
                if nxt:
                    norm_q_stats(g + 1)
                make_c(g, 0)
                if f >= 0:
                    take_x2T(f)
                if nxt:
                    norm_q(g + 1)
                if f >= 1:
                    finish(f - 1)
                if f >= 0:
                    low(f, 0)
                    low(f, 1)
                make_c(g, 1)
                if f >= 0:
                    low(f, 2)
                scaled = head_out(g, 0)
                if f >= 0:
                    low(f, 3)
                residual(g, 0, scaled)
                if nxt:
                    forget_min(g + 1)
                norm_x(g, 0)
                make_c(g, 2)
                if nxt:
                    gate_scans(g + 1)
                scaled = head_out(g, 1)
                if f >= 0:
                    low(f, 4)
                residual(g, 1, scaled)
                if f >= 0:
                    low(f, 5)
                norm_x(g, 1)
                make_c(g, 3)
                scaled = head_out(g, 2)
                if f >= 0:
                    low(f, 6)
                residual(g, 2, scaled)
                if f >= 0:
                    low(f, 7)
                norm_x(g, 2)
                scaled = head_out(g, 3)
                residual(g, 3, scaled)
                norm_x(g, 3)
            f = NG - 1
            take_x2T(f)
            finish(f - 1)
            for m in range(2 * FT):
                low(f, m)
            finish(f)

        @block.gpsimd
        def _(pool):
            own = [0]

            def step(ins):
                own[0] += 1
                ins.then_inc(pool_own, 1)
                pool.wait_ge(pool_own, own[0])

            def rstd(dst, var, work, scale):
                step(pool.tensor_scalar(work, var, LN_EPS, scale, ALU.add, ALU.mult))
                return pool.tensor_tensor(dst, work, minus_half[:, 0:dst.shape[-1]], ALU.pow)

            def q_scale(g):
                pool.wait_ge(q_stats, g + 1)
                if g >= 1:
                    pool.wait_ge(xn_ready, GB * g)
                rstd(rs_q[:, :], mv_q[:, :, 1], ve_q[:, :], 1.0).then_inc(q_rstd, 1)

            def take_values(g):
                p = g % 2
                pool.wait_ge(ctx_loaded[p], 16 * (g // 2 + 1))
                if g >= 2:
                    pool.wait_ge(pv_ready, GB * (g - 1))
                pool.tensor_copy(vals[:, p, :, :, 0:DH].rearrange("p j h d -> p (j h) d"),
                                 cs_in[:, p].rearrange("p j (h d) -> p (j h) d", d=DH)).then_inc(vals_ready, 1)

            def mask(g, j):
                pool.wait_ge(max_spread[g % 2][j], 16 * (g // 2 + 1))
                pool.affine_select(out=maxb[:, g % 2, j], in_=maxb[:, g % 2, j], compare_op=ALU.is_ge, fill=NEVER, base=0,
                                   pattern=[[0, NH], [1, S]], channel_multiplier=-1).then_inc(masked, 1)

            def h_scale(g, j):
                n = GB * g + j
                pool.wait_ge(h_stats, n + 1)
                if n >= 2:
                    pool.wait_ge(x1_ready, n - 1)
                rstd(rs_h[:, n % 2:n % 2 + 1], mv_h[:, n % 2, 1:2], ve_h[:, n % 2:n % 2 + 1], 1.0).then_inc(h_rstd, 1)

            def x_scale(g, j):
                n = GB * g + j
                pool.wait_ge(x_stats, n + 1)
                rstd(rs_x[:, n % 2:n % 2 + 1], mv_x[:, n % 2, 1:2], ve_x[:, n % 2:n % 2 + 1], X2_SCALE ** -2).then_inc(x_rstd, 1)

            def x2_take_low(g, j):
                n = GB * g + j
                pool.wait_ge(x2_high, n + 1)
                pool.tensor_tensor(x2p[:, n % 2, 1], x2[:, n % 2], x2p[:, n % 2, 0], ALU.subtract).then_inc(x2_low, 1)

            step(pool.memset(minus_half[:, :], -0.5))
            step(pool.memset(ident[:, :], 0.0))
            step(pool.affine_select(out=ident[:, :], in_=ident[:, :], compare_op=ALU.not_equal, fill=1.0, base=0,
                                    pattern=[[-1, 128]], channel_multiplier=1))
            step(pool.tensor_copy(ident16[:, :], ident[:, :]))
            step(pool.memset(odd_heads[:, :], 1.0))
            for i in range(NH // 2):
                step(pool.memset(odd_heads[32 * i:32 * i + DH, :], 0.0))
            pool.memset(vals[:, :, :, :, DH:VW], 0.0).then_inc(pool_own, 1)
            own[0] += 1
            pool.wait_ge(pool_own, own[0])
            pool.memset(vals[:, :, :, :, ONE:ONE + 1], 1.0).then_inc(consts_ready, 1)
            pool.wait_ge(consts_ready, 1)
            q_scale(0)
            take_values(0)
            mask(0, 0)
            mask(0, 1)
            for g in range(NG):
                f = g - 1
                nxt = g + 1 < NG
                mask(g, 2)
                if f >= 0:
                    x2_take_low(f, GB - 1)
                if nxt:
                    q_scale(g + 1)
                    take_values(g + 1)
                mask(g, 3)
                h_scale(g, 0)
                x_scale(g, 0)
                x2_take_low(g, 0)
                h_scale(g, 1)
                x_scale(g, 1)
                x2_take_low(g, 1)
                if nxt:
                    mask(g + 1, 0)
                h_scale(g, 2)
                x_scale(g, 2)
                x2_take_low(g, 2)
                if nxt:
                    mask(g + 1, 1)
                h_scale(g, 3)
                x_scale(g, 3)
            x2_take_low(NG - 1, GB - 1)


_INS = ['x', 'ctx_1024', 'L0_xattn_igate_w', 'L0_xattn_igate_b', 'L0_xattn_fgate_w', 'L0_xattn_fgate_b',
        'L0_xattn_ln_scale', 'L0_ffn_k0', 'L0_ffn_k1', 'L0_ffn_k2', 'L0_ffn_s0', 'L0_ffn_s1', 'L0_ffn_s2']


def kernel(**inputs):
    import numpy as np
    import concourse.bacc as bacc
    from concourse.bass_utils import run_bass_kernel_spmd

    nc = bacc.Bacc("TRN2", target_bir_lowering=False, num_devices=1)
    arrays, args = {}, []
    for name in _INS:
        a = np.ascontiguousarray(inputs[name])
        arrays[f"in_{name}"] = a
        args.append(nc.dram_tensor(f"in_{name}", a.shape, mybir.dt.from_np(a.dtype), kind="ExternalInput").ap())
    running_max = nc.dram_tensor("running_max", [NG, GB, NH, S], F32, kind="Internal").ap()
    out = nc.dram_tensor("out", [B, S, D], F32, kind="ExternalOutput").ap()
    xattn_ffn(nc, *args, running_max, out)
    result = run_bass_kernel_spmd(nc, [arrays], core_ids=[0])
    return result.results[0]["out"]
```

```python
from contextlib import ExitStack

import concourse.bass as bass
from concourse import mybir

F32 = mybir.dt.float32
F16 = mybir.dt.float16
U8 = mybir.dt.uint8
ALU = mybir.AluOpType
ACT = mybir.ActivationFunctionType

B, S, D = 16, 128, 128
NH = 8
DH = D // NH
GB = 4
NG = B // GB
FG = 2
NF = B // FG
FFN_LAG = 5
SLOTS = B + FFN_LAG + 2
FB = 3
F = 512
FT = F // 128
VW = 32
ONE = DH
TOK = FG * S
XR = 3 * GB
LN_EPS = 1e-5
EPS = 1e-6
LOWEST = -3.0e38
NEVER = 1e30
QK_SCALE = 1.0 / DH ** 0.5
X2_SCALE = 2.0 ** 12
W0_SCALE = 2.0 ** -4
W1_SCALE = 2.0 ** -9
OUT_SCALE = 8.0 / (X2_SCALE * W0_SCALE * W1_SCALE)


def ffn_of_slot(n):
    f, r = divmod(n - FFN_LAG, FG)
    early, late = (([(f - 1, 6), (f - 1, 7)], [(f, 0), (f, 1)]),
                   ([(f - 1, 8), (f, 2), (f, 3)], [(f, 4), (f, 5)]))[r]
    return tuple([(i, m) for i, m in part if 0 <= i < NF] for part in (early, late))


SUMS = [at for n in range(SLOTS) for part in ffn_of_slot(n) for at in part]
HIDDEN_SUMS = [at for at in SUMS if at[1] < 2 * FT]


def sums_to(f, m):
    return SUMS.index((f, m)) + 1


def hidden_to(f, m):
    return HIDDEN_SUMS.index((f, m)) + 1


def xattn_ffn(nc, x, ctx_in, igate_w, igate_b, fgate_w, fgate_b, ln_scale, k0, k1, k2, s0, s1, s2, running_max, out):
    with ExitStack() as stack:
        def sb(name, shape, dt=F32):
            return stack.enter_context(nc.sbuf_tensor(name, shape, dt))

        def ps(name, shape, dt=F32):
            return stack.enter_context(nc.psum_tensor(name, shape, dt))

        def sem(name):
            return stack.enter_context(nc.semaphore(name))

        ident = sb("ident", [128, 128])
        ident16 = sb("ident16", [128, 128], F16)
        gate_rows = sb("gate_rows", [2 * NH, 3 * D])
        wq = sb("wq", [128, 2, VW])
        wkv = sb("wkv", [128, 2, VW])
        bias_in = sb("bias_in", [NH, 2])
        gate_b = sb("gate_b", [128, 2])
        lns = sb("lns", [128, D])
        minus_half = sb("minus_half", [128, 1])
        s_in = sb("s_in", [128, 3])
        s_work = sb("s_work", [128, 8])
        k0_in = sb("k0_in", [128, 2, F], U8)
        k1_in = sb("k1_in", [128, FT, F], U8)
        k2_in = sb("k2_in", [128, FT, D], U8)
        w0 = sb("w0", [128, F], F16)
        w1 = sb("w1", [128, FT, F], F16)
        w2 = sb("w2", [128, FT, D], F16)
        xs = sb("xs", [128, B, D])
        cs_in = sb("cs_in", [128, B, D])
        vals = sb("vals", [128, 2, GB, NH, VW])
        xn = sb("xn", [128, 2 * GB, D])
        st_q = sb("st_q", [128, GB, 6])
        mv_q = sb("mv_q", [128, GB, 2])
        ve_q = sb("ve_q", [128, GB])
        rs_q = sb("rs_q", [128, GB])
        qcT = sb("qcT", [128, 2, GB, 2, S])
        q_heads = sb("q_heads", [128, 2, GB, NH, S])
        f_min = sb("f_min", [128, S])
        f_abs = sb("f_abs", [128, S])
        f_exp = sb("f_exp", [128, S])
        f_ln = sb("f_ln", [128, S])
        cumf = sb("cumf", [128, S])
        a_row = sb("a_row", [128, S])
        max_row = sb("max_row", [128, 2, S])
        m_row = sb("m_row", [128, S])
        aT = sb("aT", [128, 2, GB, VW])
        em = sb("em", [128, 2, GB, VW])
        maxb = sb("maxb", [128, 2, GB, NH, S])
        dmat = sb("dmat", [128, 2, NH, S])
        cmat = sb("cmat", [128, 2, NH, S])
        oT = sb("oT", [128, 2, 2, S])
        den = sb("den", [128, 2, NH])
        hatt = sb("hatt", [128, 2, D])
        st_h = sb("st_h", [128, 2, 6])
        mv_h = sb("mv_h", [128, 2, 2])
        ve_h = sb("ve_h", [128, 2])
        rs_h = sb("rs_h", [128, 2])
        hsc = sb("hsc", [128, 2, D])
        x1 = sb("x1", [128, XR, D])
        st_x = sb("st_x", [128, 2, 6])
        mv_x = sb("mv_x", [128, 2, 2])
        ve_x = sb("ve_x", [128, 2])
        rs_x = sb("rs_x", [128, 2])
        x2 = sb("x2", [128, 2, D])
        x2p = sb("x2p", [128, 2, 2, D], F16)
        x2T = sb("x2T", [128, 2, 2, TOK], F16)
        h1 = sb("h1", [128, FT, 2, TOK], F16)
        h2 = sb("h2", [128, FT, 2, TOK], F16)
        outb = sb("outb", [128, 2, FG, D])
        pG = ps("pG", [128, 4, S])
        pS = ps("pS", [128, NH, S])
        pO = ps("pO", [128, 4, S])
        pX = ps("pX", [128, 2, 2, TOK], F16)
        pF = [ps(f"pF{i}", [128, TOK], F32) for i in range(FB)]

        ctx_loaded = [sem(f"ctx_loaded{g}") for g in range(NG)]
        x_loaded = [sem(f"x_loaded{g}") for g in range(NG)]
        gatew_loaded = sem("gatew_loaded")
        ffnw_loaded = sem("ffnw_loaded")
        lns_loaded = sem("lns_loaded")
        consts_ready = sem("consts_ready")
        q_heads_cleared = sem("q_heads_cleared")
        cleared = sem("cleared")
        gatew_turned = sem("gatew_turned")
        gatew_ready = sem("gatew_ready")
        ffnw_ready = sem("ffnw_ready")
        q_stats = sem("q_stats")
        q_rstd = sem("q_rstd")
        xn_ready = sem("xn_ready")
        vals_ready = sem("vals_ready")
        turned = sem("turned")
        turned_out = sem("turned_out")
        gates_ready = sem("gates_ready")
        f_min_ready = sem("f_min_ready")
        f_ln_ready = sem("f_ln_ready")
        max_ready = sem("max_ready")
        m_ready = sem("m_ready")
        am_turned = sem("am_turned")
        am_ready = sem("am_ready")
        max_stored = sem("max_stored")
        max_spread = [[sem(f"max_spread{p}{j}") for j in range(GB)] for p in range(2)]
        heads_spread = [sem(f"heads_spread{p}") for p in range(2)]
        scores_ready = sem("scores_ready")
        exp_ready = sem("exp_ready")
        masked = sem("masked")
        c_ready = sem("c_ready")
        pv_ready = sem("pv_ready")
        oT_ready = sem("oT_ready")
        o_turned = sem("o_turned")
        o_read = sem("o_read")
        h_stats = sem("h_stats")
        h_centre = sem("h_centre")
        h_rstd = sem("h_rstd")
        x_stats = sem("x_stats")
        x_rstd = sem("x_rstd")
        x1_ready = sem("x1_ready")
        x2_ready = sem("x2_ready")
        x2_high = sem("x2_high")
        x2_low = sem("x2_low")
        x2_turned = sem("x2_turned")
        x2T_ready = sem("x2T_ready")
        ffn_sums = sem("ffn_sums")
        ffn_high = sem("ffn_high")
        ffn_low = sem("ffn_low")
        out_ready = sem("out_ready")
        out_stored = [sem(f"out_stored{p}") for p in range(2)]
        dve_own = sem("dve_own")
        act_own = sem("act_own")
        pool_own = sem("pool_own")

        def group_rows(dram, g):
            return dram[GB * g:GB * (g + 1)].rearrange("b s d -> s b d")

        def store(sp, f):
            sp.wait_ge(out_ready, f + 1)
            sp.dma_start(out[FG * f:FG * (f + 1)].rearrange("b s d -> s b d"),
                         outb[:, f % 2]).then_inc(out_stored[f % 2], 16)

        block = stack.enter_context(nc.Block())

        @block.sync
        def _(sp):
            def load_x(g):
                sp.dma_start(xs[:, GB * g:GB * (g + 1)], group_rows(x, g)).then_inc(x_loaded[g], 16)

            def load_ctx(g):
                sp.dma_start(cs_in[:, GB * g:GB * (g + 1)], group_rows(ctx_in, g)).then_inc(ctx_loaded[g], 16)

            load_x(0)
            for n, bias in enumerate((igate_b, fgate_b)):
                sp.dma_start(bias_in[:, n:n + 1], bias.rearrange("(h a) -> h a", a=1)).then_inc(gatew_loaded, 16)
            load_x(1)
            load_ctx(1)
            for k_dram, k_in in ((k0, k0_in), (k1, k1_in), (k2, k2_in)):
                sp.dma_start(k_in[:, :, :], k_dram.rearrange("(c p) n -> p c n", p=128)).then_inc(ffnw_loaded, 16)
            load_x(2)

            def spread_heads(g):
                sp.wait_ge(q_heads_cleared, g % 2 + 1)
                if g >= 2:
                    sp.wait_ge(scores_ready, 2 * GB * (g - 1))
                sp.wait_ge(turned_out, GB // 2 * (g + 1))
                for h in range(NH):
                    sp.dma_start(q_heads[DH * h:DH * (h + 1), g % 2, :, h],
                                  qcT[DH * h:DH * (h + 1), g % 2, :, 0]).then_inc(heads_spread[g % 2], 16)

            for g in range(NG):
                spread_heads(g)
                p = g % 2
                sp.wait_ge(max_ready, g + 1)
                sp.dma_start(running_max[g], max_row[:, p, :]).then_inc(max_stored, 16)
                sp.wait_ge(max_stored, 16 * (g + 1))
                if g >= 2:
                    sp.wait_ge(exp_ready, GB * (g - 1))
                for j in range(GB):
                    sp.dma_start(maxb[:, p, j],
                                 running_max[g:g + 1, 32 * j:32 * j + NH].broadcast_to([128, NH, S])).then_inc(max_spread[p][j], 16)
                if g == 0:
                    load_ctx(2)
                    load_x(3)
                    load_ctx(3)
            for f in range(NF):
                store(sp, f)
            for p in range(2):
                sp.wait_ge(out_stored[p], 16 * (NF // 2))

        @block.tensor
        def _(pe):
            def turn(pair):
                n = 2 * pair
                g = n // GB
                if n % GB == 0:
                    pe.wait_ge(ctx_loaded[g], 16)
                pe.wait_ge(xn_ready, n + 2)
                if pair == 0:
                    pe.wait_ge(gatew_ready, 1)
                elif pair % 2 == 0:
                    pe.wait_ge(am_ready, g)
                else:
                    pe.wait_ge(turned_out, pair)
                for i in range(2):
                    pe.transpose(pG[:, 2 * i], xn[:, (n + i) % (2 * GB)], ident[:, :])
                    last = pe.transpose(pG[:, 2 * i + 1], cs_in[:, n + i], ident[:, :])
                last.then_inc(turned, 1)

            def gates(g):
                pe.wait_ge(turned_out, GB // 2 * (g + 1))
                for n in range(2):
                    for part, w in enumerate((wq, wkv)):
                        for j in range(GB):
                            last = pe.matmul(pG[32 * j:32 * j + VW, n], w[:, n, :], qcT[:, g % 2, j, part],
                                             start=(part == 0), stop=(part == 1))
                last.then_inc(gates_ready, 1)

            def turn_am(g):
                pe.wait_ge(m_ready, g + 1)
                pe.transpose(pG[:, 2], a_row[:, :], ident[:, :])
                pe.transpose(pG[:, 3], m_row[:, :], ident[:, :]).then_inc(am_turned, 1)

            def scores(n):
                g, j = divmod(n, GB)
                if j == 0:
                    pe.wait_ge(heads_spread[g % 2], 16 * NH * (g // 2 + 1))
                for half in range(2):
                    if n >= 1:
                        pe.wait_ge(c_ready, 2 * (n - 1) + half + 1)
                    pe.matmul(pS[:, 4 * half:4 * half + 4].rearrange("p h s -> p (h s)"), qcT[:, g % 2, j, 1],
                              q_heads[:, g % 2, j, 4 * half:4 * half + 4].rearrange("p h s -> p (h s)"),
                              start=True, stop=True).then_inc(scores_ready, 1)

            def weigh(n):
                pe.wait_ge(vals_ready, n + 1)
                if n >= 1:
                    pe.wait_ge(o_read, n)
                for half in range(2):
                    pe.wait_ge(c_ready, 2 * n + half + 1)
                    for i in range(4):
                        h = 4 * half + i
                        last = pe.matmul(pO[32 * i:32 * i + VW, half], vals[:, n // GB % 2, n % GB, h],
                                         cmat[:, n % 2, h], start=True, stop=True)
                last.then_inc(pv_ready, 1)

            def turn_o(n):
                pe.wait_ge(oT_ready, n + 1)
                for half in range(2):
                    last = pe.transpose(pO[:, 2 + half], oT[:, n % 2, half], ident[:, :])
                last.then_inc(o_turned, 1)

            def turn_x2(n):
                f, j = divmod(n, FG)
                if j == 0 and f >= 2:
                    pe.wait_ge(x2T_ready, f - 1)
                pe.wait_ge(x2_high, n + 1)
                pe.wait_ge(x2_low, n + 1)
                for part in range(2):
                    last = pe.transpose(pX[:, f % 2, part, S * j:S * (j + 1)], x2p[:, n % 2, part], ident16[:, :])
                last.then_inc(x2_turned, 1)

            def ffn(f, m):
                at = SUMS.index((f, m))
                if at >= FB:
                    f_before, m_before = SUMS[at - FB]
                    if m_before == 2 * FT:
                        pe.wait_ge(out_ready, f_before + 1)
                    else:
                        pe.wait_ge(ffn_low, hidden_to(f_before, m_before))
                bank = pF[at % FB][:, 0:TOK]
                if m < FT:
                    if m == 0:
                        pe.wait_ge(ffnw_ready, 1)
                        pe.wait_ge(x2T_ready, f + 1)
                    for part in range(2):
                        last = pe.matmul(bank, w0[:, 128 * m:128 * (m + 1)], x2T[:, f % 2, part],
                                         start=(part == 0), stop=(part == 1))
                elif m < 2 * FT:
                    for k in range(FT):
                        pe.wait_ge(ffn_low, hidden_to(f, k))
                        for part in range(2):
                            last = pe.matmul(bank, w1[:, k, 128 * (m - FT):128 * (m - FT + 1)], h1[:, k, part],
                                             start=(k == 0 and part == 0), stop=(k == FT - 1 and part == 1))
                else:
                    pe.wait_ge(ffn_low, hidden_to(f, 2 * FT - 1))
                    for j in range(FG):
                        for k in range(FT):
                            for part in range(2):
                                last = pe.matmul(bank[:, D * j:D * (j + 1)], h2[:, k, part, S * j:S * (j + 1)],
                                                 w2[:, k], start=(k == 0 and part == 0),
                                                 stop=(k == FT - 1 and part == 1))
                last.then_inc(ffn_sums, 1)

            pe.wait_ge(consts_ready, 1)
            pe.wait_ge(gatew_loaded, 16 * 4)
            for part in range(3):
                last = pe.transpose(pG[:, part, 0:2 * NH], gate_rows[:, D * part:D * (part + 1)],
                                    ident[0:2 * NH, 0:2 * NH])
            for j in range(GB):
                last = pe.matmul(pG[32 * j:32 * j + VW, 3, 0:2], ident[0:NH, 0:VW], bias_in[:, :], start=True, stop=True)
            last.then_inc(gatew_turned, 1)
            turn(0)
            turn(1)
            gates(0)
            turn_am(0)
            turn(2)
            turn(3)
            for n in range(SLOTS):
                g, k = divmod(n, GB)
                prepare = n < B and g + 1 < NG
                early, late = ffn_of_slot(n)
                if prepare and k == 0:
                    gates(g + 1)
                if n < B:
                    scores(n)
                if prepare and k == 1:
                    turn_am(g + 1)
                if k == 3 and g + 2 < NG:
                    turn(2 * (g + 2))
                if 0 <= n - 1 < B:
                    weigh(n - 1)
                if 0 <= n - 4 < B:
                    turn_x2(n - 4)
                if k == 3 and g + 2 < NG:
                    turn(2 * (g + 2) + 1)
                for f, m in early:
                    ffn(f, m)
                if 0 <= n - 1 < B:
                    turn_o(n - 1)
                for f, m in late:
                    ffn(f, m)

        @block.scalar
        def _(act):
            own = [0]

            def step(ins):
                own[0] += 1
                ins.then_inc(act_own, 1)
                act.wait_ge(act_own, own[0])

            def turn_out(pair):
                g, j = divmod(2 * pair, GB)
                act.wait_ge(turned, pair + 1)
                if j == 0 and g >= 2:
                    act.wait_ge(scores_ready, 2 * GB * (g - 1))
                act.copy(qcT[:, g % 2, j:j + 2].rearrange("p j a s -> p (j a) s"), pG[:, :]).then_inc(turned_out, 1)

            def gate_logs(g):
                act.wait_ge(f_min_ready, g + 1)
                step(act.activation(f_abs[:, :], pG[:, 1], ACT.Abs, bias=gate_b[:, 1:2]))
                step(act.activation(f_exp[:, :], f_abs[:, :], ACT.Exp, scale=-1.0))
                act.activation(f_ln[:, :], f_exp[:, :], ACT.Ln, bias=1.0).then_inc(f_ln_ready, 1)

            def gate_out(g):
                act.wait_ge(am_turned, g + 1)
                if g >= 2:
                    act.wait_ge(o_read, GB * (g - 1))
                act.copy(aT[:, g % 2].rearrange("p j h -> p (j h)"), pG[:, 2])
                e = em[:, g % 2].rearrange("p j h -> p (j h)")
                step(act.activation(e, pG[:, 3], ACT.Exp, scale=-1.0))
                act.activation(e, e, ACT.Copy, bias=EPS).then_inc(am_ready, 1)

            def decay(n, heads):
                if n >= B:
                    return
                g, j = divmod(n, GB)
                if heads[0] == 0:
                    act.wait_ge(am_ready, g + 1)
                    act.wait_ge(masked, n + 1)
                    if n >= 2:
                        act.wait_ge(c_ready, 2 * (n - 1))
                for h in heads:
                    last = act.activation(dmat[:, n % 2, h], maxb[:, g % 2, j, h], ACT.Exp,
                                          bias=aT[:, g % 2, j, h:h + 1], scale=-1.0)
                if heads[-1] == NH - 1:
                    last.then_inc(exp_ready, 1)

            def take_o(n):
                act.wait_ge(pv_ready, n + 1)
                if n >= 2:
                    act.wait_ge(o_turned, n - 1)
                act.copy(oT[:, n % 2], pO[:, 0:2]).then_inc(oT_ready, 1)

            def x2_take_high(n):
                act.wait_ge(x2_ready, n + 1)
                if n >= 2:
                    act.wait_ge(x2_turned, n - 1)
                act.copy(x2p[:, n % 2, 0], x2[:, n % 2]).then_inc(x2_high, 1)

            def high(f, m):
                if m == 2 * FT:
                    return
                act.wait_ge(ffn_sums, sums_to(f, m))
                dst = h1 if m < FT else h2
                act.activation(dst[:, m % FT, 0], pF[SUMS.index((f, m)) % FB][:, 0:TOK], ACT.Relu).then_inc(ffn_high, 1)

            act.preload_act_table_set("natural_log_exp_and_others")
            act.dma_start(cs_in[:, 0:GB], group_rows(ctx_in, 0)).then_inc(ctx_loaded[0], 16)
            act.dma_start(gate_rows[0:NH, :], igate_w).then_inc(gatew_loaded, 16)
            act.dma_start(gate_rows[NH:2 * NH, :], fgate_w).then_inc(gatew_loaded, 16)
            act.dma_start(lns[:, :], ln_scale.rearrange("(a d) -> a d", a=1).broadcast_to([128, D])).then_inc(lns_loaded, 16)
            for i, s in enumerate((s0, s1, s2)):
                act.dma_start(s_in[:, i:i + 1], s.rearrange("(a d) -> a d", a=1).broadcast_to([128, 1])).then_inc(ffnw_loaded, 16)
            act.wait_ge(consts_ready, 1)
            turn_out(0)
            turn_out(1)
            gate_logs(0)
            gate_out(0)
            turn_out(2)
            turn_out(3)
            decay(0, range(NH))
            for n in range(SLOTS):
                g, k = divmod(n, GB)
                prepare = n < B and g + 1 < NG
                for f, m in ffn_of_slot(n - 1)[1]:
                    high(f, m)
                if prepare and k == 0:
                    gate_logs(g + 1)
                if prepare and k == 1:
                    gate_out(g + 1)
                decay(n + 1, range(0, 3))
                if k == 3 and g + 2 < NG:
                    turn_out(2 * (g + 2))
                if 0 <= n - 1 < B:
                    take_o(n - 1)
                if k == 3 and g + 2 < NG:
                    turn_out(2 * (g + 2) + 1)
                for f, m in ffn_of_slot(n)[0]:
                    high(f, m)
                if 0 <= n - 3 < B:
                    x2_take_high(n - 3)
                decay(n + 1, range(3, NH))

        @block.vector
        def _(dve):
            own = [0]

            def mark(ins):
                own[0] += 1
                ins.then_inc(dve_own, 1)
                return own[0]

            def step(ins):
                dve.wait_ge(dve_own, mark(ins))

            def q_statistics(n):
                if n >= B:
                    return None
                if n % GB == 0:
                    dve.wait_ge(x_loaded[n // GB], 16)
                return mark(dve.bn_stats(st_q[:, n % GB], xs[:, n]))

            def q_moments(n, stats):
                if n >= B:
                    return
                dve.wait_ge(dve_own, stats)
                if n >= GB:
                    dve.wait_ge(q_rstd, n - GB + 1)
                dve.bn_aggr(mv_q[:, n % GB], st_q[:, n % GB]).then_inc(q_stats, 1)

            def norm_q(n):
                if n >= B:
                    return
                dve.wait_ge(q_rstd, n + 1)
                dve.wait_ge(q_stats, n + 1)
                if n >= 2 * GB and n % 2 == 0:
                    dve.wait_ge(turned, (n - 2 * GB) // 2 + 1)
                dve.tensor_scalar(xn[:, n % (2 * GB)], xs[:, n], mv_q[:, n % GB, 0:1], rs_q[:, n % GB:n % GB + 1],
                                  ALU.subtract, ALU.mult).then_inc(xn_ready, 1)

            def forget_min(g):
                dve.wait_ge(gates_ready, g + 1)
                dve.tensor_scalar(f_min[:, :], pG[:, 1], gate_b[:, 1:2], 0.0, ALU.add, ALU.min).then_inc(f_min_ready, 1)

            def gate_scans(g):
                dve.wait_ge(f_ln_ready, g + 1)
                dve.wait_ge(f_min_ready, g + 1)
                step(dve.tensor_tensor_scan(cumf[:, :], f_min[:, :], f_ln[:, :], 0.0, ALU.add, ALU.subtract))
                if g >= 1:
                    dve.wait_ge(am_turned, g)
                step(dve.scalar_tensor_tensor(out=a_row[:, :], in0=pG[:, 0], scalar=gate_b[:, 0:1], in1=cumf[:, :],
                                              op0=ALU.add, op1=ALU.subtract))
                if g >= 2:
                    dve.wait_ge(max_stored, 16 * (g - 1))
                dve.tensor_tensor_scan(max_row[:, g % 2], a_row[:, :], a_row[:, :], LOWEST,
                                       ALU.max, ALU.max).then_inc(max_ready, 1)
                dve.wait_ge(max_ready, g + 1)
                dve.tensor_tensor(m_row[:, :], cumf[:, :], max_row[:, g % 2], ALU.add).then_inc(m_ready, 1)

            def make_c(n):
                dve.wait_ge(exp_ready, n + 1)
                if n >= 2:
                    dve.wait_ge(pv_ready, n - 1)
                for half in range(2):
                    part = slice(4 * half, 4 * half + 4)
                    dve.wait_ge(scores_ready, 2 * n + half + 1)
                    dve.scalar_tensor_tensor(out=cmat[:, n % 2, part].rearrange("p h s -> p (h s)"),
                                             in0=pS[:, part].rearrange("p h s -> p (h s)"), scalar=QK_SCALE,
                                             in1=dmat[:, n % 2, part].rearrange("p h s -> p (h s)"),
                                             op0=ALU.mult, op1=ALU.mult).then_inc(c_ready, 1)

            def by_head(n):
                return pO[:, 2:4].rearrange("p a (i v) -> p (a i) v", v=VW)

            def normalizer_1(n):
                dve.wait_ge(o_turned, n + 1)
                dve.wait_ge(am_ready, n // GB + 1)
                return mark(dve.scalar_tensor_tensor(out=den[:, n % 2], in0=by_head(n)[:, :, ONE], scalar=EPS,
                                                     in1=em[:, n // GB % 2, n % GB, 0:NH],
                                                     op0=ALU.subtract, op1=ALU.max, reverse0=True))

            def normalizer_2(n, before):
                dve.wait_ge(dve_own, before)
                return mark(dve.scalar_tensor_tensor(out=den[:, n % 2], in0=by_head(n)[:, :, ONE], scalar=EPS,
                                                     in1=den[:, n % 2], op0=ALU.add, op1=ALU.max))

            def normalizer_3(n, before):
                dve.wait_ge(dve_own, before)
                return mark(dve.reciprocal(den[:, n % 2], den[:, n % 2]))

            def head_out(n, before):
                dve.wait_ge(dve_own, before)
                dve.tensor_tensor(hatt[:, n % 2].rearrange("p (h d) -> p h d", d=DH), by_head(n)[:, :, 0:DH],
                                  den[:, n % 2].unsqueeze(2).broadcast_to([128, NH, DH]), ALU.mult).then_inc(o_read, 1)

            def h_statistics(n):
                dve.wait_ge(o_read, n + 1)
                return mark(dve.bn_stats(st_h[:, n % 2], hatt[:, n % 2]))

            def h_moments(n, before):
                dve.wait_ge(dve_own, before)
                dve.bn_aggr(mv_h[:, n % 2], st_h[:, n % 2]).then_inc(h_stats, 1)

            def h_centred(n):
                if n == 0:
                    dve.wait_ge(lns_loaded, 16)
                dve.wait_ge(h_stats, n + 1)
                dve.scalar_tensor_tensor(out=hsc[:, n % 2], in0=hatt[:, n % 2], scalar=mv_h[:, n % 2, 0:1],
                                         in1=lns[:, :], op0=ALU.subtract, op1=ALU.mult).then_inc(h_centre, 1)

            def residual(n):
                if n >= XR and n % FG == 0:
                    dve.wait_ge(out_ready, (n - XR) // FG + 1)
                dve.wait_ge(h_centre, n + 1)
                dve.wait_ge(h_rstd, n + 1)
                dve.scalar_tensor_tensor(out=x1[:, n % XR], in0=hsc[:, n % 2], scalar=rs_h[:, n % 2:n % 2 + 1],
                                         in1=xs[:, n], op0=ALU.mult, op1=ALU.add).then_inc(x1_ready, 1)

            def x_statistics(n):
                dve.wait_ge(x1_ready, n + 1)
                return mark(dve.bn_stats(st_x[:, n % 2], x1[:, n % XR]))

            def x_moments(n, before):
                dve.wait_ge(dve_own, before)
                dve.bn_aggr(mv_x[:, n % 2], st_x[:, n % 2]).then_inc(x_stats, 1)

            def norm_x(n):
                e = n % 2
                dve.wait_ge(x_rstd, n + 1)
                dve.wait_ge(x_stats, n + 1)
                if n >= 2:
                    dve.wait_ge(x2_low, n - 1)
                dve.tensor_scalar(x2[:, e], x1[:, n % XR], mv_x[:, e, 0:1], rs_x[:, e:e + 1],
                                  ALU.subtract, ALU.mult).then_inc(x2_ready, 1)

            def take_x2T(f):
                dve.wait_ge(x2_turned, FG * (f + 1))
                if f >= 2:
                    dve.wait_ge(ffn_sums, sums_to(f - 2, FT - 1))
                dve.tensor_copy(x2T[:, f % 2], pX[:, f % 2]).then_inc(x2T_ready, 1)

            def low(f, m):
                bank = pF[SUMS.index((f, m)) % FB][:, 0:TOK]
                if m == 2 * FT:
                    dve.wait_ge(ffn_sums, sums_to(f, m))
                    if f >= 2:
                        dve.wait_ge(out_stored[f % 2], 16 * (f // 2))
                    dve.scalar_tensor_tensor(out=outb[:, f % 2].rearrange("p j d -> p (j d)"), in0=bank,
                                             scalar=s_work[:, 7:8],
                                             in1=x1[:, FG * f % XR:FG * f % XR + FG].rearrange("p j d -> p (j d)"),
                                             op0=ALU.mult, op1=ALU.add).then_inc(out_ready, 1)
                    return
                dve.wait_ge(ffn_high, hidden_to(f, m))
                dst = h1 if m < FT else h2
                dve.scalar_tensor_tensor(out=dst[:, m % FT, 1], in0=bank, scalar=0.0, in1=dst[:, m % FT, 0],
                                         op0=ALU.max, op1=ALU.subtract).then_inc(ffn_low, 1)

            def ffn_weights():
                dve.wait_ge(ffnw_loaded, 16 * 6)
                step(dve.tensor_scalar(s_work[:, 0:2], s_in[:, 0:2], 0.0, 2.0, ALU.is_ge, ALU.mult))
                step(dve.tensor_scalar(s_work[:, 0:2], s_work[:, 0:2], 1.0, None, ALU.subtract))
                step(dve.tensor_tensor(s_work[:, 2:4], s_work[:, 0:2], s_in[:, 0:2], ALU.mult))
                step(dve.tensor_scalar(s_work[:, 4:5], s_work[:, 0:1], W0_SCALE, None, ALU.mult))
                step(dve.tensor_scalar(s_work[:, 5:6], s_work[:, 1:2], 2.0 * W1_SCALE, None, ALU.mult))
                step(dve.tensor_scalar(s_work[:, 6:7], s_work[:, 1:2], W1_SCALE, None, ALU.mult))
                step(dve.tensor_tensor(s_work[:, 7:8], s_work[:, 2:3], s_work[:, 3:4], ALU.mult))
                step(dve.tensor_tensor(s_work[:, 7:8], s_work[:, 7:8], s_in[:, 2:3], ALU.mult))
                step(dve.tensor_scalar(s_work[:, 7:8], s_work[:, 7:8], OUT_SCALE, None, ALU.mult))
                step(dve.tensor_tensor(w0[:, :], k0_in[:, 0], k0_in[:, 1], ALU.subtract))
                step(dve.tensor_scalar(w0[:, :], w0[:, :], s_work[:, 4:5], None, ALU.mult))
                step(dve.tensor_scalar(w1[:, :, :], k1_in[:, :, :], s_work[:, 5:6], s_work[:, 6:7],
                                       ALU.mult, ALU.subtract))
                dve.tensor_scalar(w2[:, :, :], k2_in[:, :, :], 2.0, 1.0, ALU.mult, ALU.subtract).then_inc(ffnw_ready, 1)

            def gate_cols(part):
                return pG[:, part, 0:2 * NH].rearrange("p (n h) -> p n h", n=2)

            step(dve.memset(wq[:, :, :], 0.0))
            dve.memset(wkv[:, :, :], 0.0).then_inc(cleared, 1)
            dve.wait_ge(cleared, 1)
            def q_group(g):
                at = q_statistics(GB * g)
                for n in range(GB * g, GB * (g + 1)):
                    after = q_statistics(n + 1) if n + 1 < GB * (g + 1) else None
                    q_moments(n, at)
                    at = after

            def norm_group(g):
                for n in range(GB * g, GB * (g + 1)):
                    norm_q(n)

            q_group(0)
            dve.wait_ge(gatew_turned, 1)
            step(dve.tensor_copy(gate_b[:, :], pG[:, 3, 0:2]))
            step(dve.tensor_copy(wq[:, :, 0:NH], gate_cols(0)))
            step(dve.tensor_copy(wkv[:, :, 0:NH], gate_cols(1)))
            dve.tensor_tensor(wkv[:, :, 0:NH], gate_cols(2), wkv[:, :, 0:NH], ALU.add).then_inc(gatew_ready, 1)
            norm_group(0)
            q_group(1)
            norm_group(1)
            forget_min(0)
            gate_scans(0)
            ffn_weights()
            for n in range(2 * GB, 2 * GB + 2):
                q_moments(n, q_statistics(n))
            norm_q(2 * GB)
            for n in range(SLOTS):
                g, k = divmod(n, GB)
                prepare = n < B and g + 1 < NG
                before = ffn_of_slot(n - 1)[1]
                early, late = ffn_of_slot(n)
                behind = 0 <= n - 1 < B
                for f, m in before:
                    low(f, m)
                if prepare and k == 0:
                    forget_min(g + 1)
                if n < B:
                    make_c(n)
                if 0 <= n - 3 < B:
                    norm_x(n - 3)
                if 0 <= n - 2 < B:
                    residual(n - 2)
                q_at = q_statistics(n + 2 * GB + 2)
                if 0 <= n - 2 < B:
                    x_at = x_statistics(n - 2)
                if prepare and k == 0:
                    gate_scans(g + 1)
                if (n - FFN_LAG) % FG == 0 and 0 <= n - FFN_LAG < B:
                    take_x2T((n - FFN_LAG) // FG)
                for f, m in early:
                    low(f, m)
                if behind:
                    at = normalizer_1(n - 1)
                norm_q(n + 2 * GB + 1)
                if behind:
                    at = normalizer_2(n - 1, at)
                q_moments(n + 2 * GB + 2, q_at)
                if 0 <= n - 2 < B:
                    x_moments(n - 2, x_at)
                if behind:
                    at = normalizer_3(n - 1, at)
                    head_out(n - 1, at)
                if behind:
                    at = h_statistics(n - 1)
                if behind:
                    h_moments(n - 1, at)
                if behind:
                    h_centred(n - 1)

        @block.gpsimd
        def _(pool):
            own = [0]

            def step(ins):
                own[0] += 1
                ins.then_inc(pool_own, 1)
                pool.wait_ge(pool_own, own[0])

            def rstd(dst, var, work, scale):
                step(pool.tensor_scalar(work, var, LN_EPS, scale, ALU.add, ALU.mult))
                return pool.tensor_tensor(dst, work, minus_half[:, :], ALU.pow)

            def q_scale(n, count=1):
                if n >= B:
                    return
                e = n % GB
                pool.wait_ge(q_stats, n + count)
                if n >= GB:
                    pool.wait_ge(xn_ready, n + count - GB)
                step(pool.tensor_scalar(ve_q[:, e:e + count], mv_q[:, e:e + count, 1], LN_EPS, None, ALU.add))
                pool.tensor_tensor(rs_q[:, e:e + count], ve_q[:, e:e + count],
                                   minus_half[:, :].broadcast_to([128, count]), ALU.pow).then_inc(q_rstd, count)

            def take_values(n):
                if n >= B:
                    return
                g, j = divmod(n, GB)
                if j == 0:
                    pool.wait_ge(ctx_loaded[g], 16)
                if n >= 2 * GB:
                    pool.wait_ge(pv_ready, n - 2 * GB + 1)
                pool.tensor_copy(vals[:, g % 2, j, :, 0:DH], cs_in[:, n].rearrange("p (h d) -> p h d", d=DH)).then_inc(vals_ready, 1)

            def mask(n):
                if n >= B:
                    return
                g, j = divmod(n, GB)
                pool.wait_ge(max_spread[g % 2][j], 16 * (g // 2 + 1))
                pool.affine_select(out=maxb[:, g % 2, j], in_=maxb[:, g % 2, j], compare_op=ALU.is_ge, fill=NEVER,
                                   base=0, pattern=[[0, NH], [1, S]], channel_multiplier=-1).then_inc(masked, 1)

            def h_scale(n):
                e = n % 2
                pool.wait_ge(h_stats, n + 1)
                if n >= 2:
                    pool.wait_ge(x1_ready, n - 1)
                rstd(rs_h[:, e:e + 1], mv_h[:, e, 1:2], ve_h[:, e:e + 1], 1.0).then_inc(h_rstd, 1)

            def x_scale(n):
                e = n % 2
                pool.wait_ge(x_stats, n + 1)
                if n >= 2:
                    pool.wait_ge(x2_ready, n - 1)
                rstd(rs_x[:, e:e + 1], mv_x[:, e, 1:2], ve_x[:, e:e + 1], X2_SCALE ** -2).then_inc(x_rstd, 1)

            def x2_take_low(n):
                pool.wait_ge(x2_high, n + 1)
                pool.tensor_tensor(x2p[:, n % 2, 1], x2[:, n % 2], x2p[:, n % 2, 0], ALU.subtract).then_inc(x2_low, 1)

            step(pool.memset(minus_half[:, :], -0.5))
            step(pool.memset(ident[:, :], 0.0))
            step(pool.affine_select(out=ident[:, :], in_=ident[:, :], compare_op=ALU.not_equal, fill=1.0, base=0,
                                    pattern=[[-1, 128]], channel_multiplier=1))
            step(pool.tensor_copy(ident16[:, :], ident[:, :]))
            step(pool.memset(vals[:, :, :, :, DH:VW], 0.0))
            pool.memset(vals[:, :, :, :, ONE:ONE + 1], 1.0).then_inc(consts_ready, 1)
            pool.wait_ge(consts_ready, 1)
            q_scale(0, GB)
            pool.memset(q_heads[:, 0], 0.0).then_inc(q_heads_cleared, 1)
            q_scale(GB, GB)
            pool.memset(q_heads[:, 1], 0.0).then_inc(q_heads_cleared, 1)
            for n in range(GB):
                take_values(n)
            mask(0)
            mask(1)
            q_scale(2 * GB)
            q_scale(2 * GB + 1)
            for n in range(SLOTS):
                if n % GB != 2:
                    mask(n + 2)
                if 0 <= n - 3 < B:
                    x2_take_low(n - 3)
                if n % GB == 2:
                    mask(n + 2)
                q_scale(n + 2 * GB + 2)
                if 0 <= n - 2 < B:
                    x_scale(n - 2)
                take_values(n + GB)
                if 0 <= n - 1 < B:
                    h_scale(n - 1)


_INS = ['x', 'ctx_1024', 'L0_xattn_igate_w', 'L0_xattn_igate_b', 'L0_xattn_fgate_w', 'L0_xattn_fgate_b',
        'L0_xattn_ln_scale', 'L0_ffn_k0', 'L0_ffn_k1', 'L0_ffn_k2', 'L0_ffn_s0', 'L0_ffn_s1', 'L0_ffn_s2']


def kernel(**inputs):
    import numpy as np
    import concourse.bacc as bacc
    from concourse.bass_utils import run_bass_kernel_spmd

    nc = bacc.Bacc("TRN2", target_bir_lowering=False, num_devices=1)
    arrays, args = {}, []
    for name in _INS:
        a = np.ascontiguousarray(inputs[name])
        arrays[f"in_{name}"] = a
        args.append(nc.dram_tensor(f"in_{name}", a.shape, mybir.dt.from_np(a.dtype), kind="ExternalInput").ap())
    running_max = nc.dram_tensor("running_max", [NG, 128, S], F32, kind="Internal").ap()
    out = nc.dram_tensor("out", [B, S, D], F32, kind="ExternalOutput").ap()
    xattn_ffn(nc, *args, running_max, out)
    result = run_bass_kernel_spmd(nc, [arrays], core_ids=[0])
    return result.results[0]["out"]
```

```python
from contextlib import ExitStack

import concourse.bass as bass
from concourse import mybir

F32 = mybir.dt.float32
F16 = mybir.dt.float16
U8 = mybir.dt.uint8
ALU = mybir.AluOpType
ACT = mybir.ActivationFunctionType

B, S, D = 16, 128, 128
NH = 8
DH = D // NH
GB = 4
NG = B // GB
FG = 2
NF = B // FG
FFN_LAG = 5
SLOTS = B + FFN_LAG + 2
F = 512
FT = F // 128
FU = 2
FB = 3
LAST = 2 * FT // FU
VW = 32
ONE = DH
TOK = FG * S
XR = 3 * GB
LN_EPS = 1e-5
EPS = 1e-6
LOWEST = -3.0e38
DIRECT = (0, 1)
NEVER = 1e30
QK_SCALE = 1.0 / DH ** 0.5
X2_SCALE = 2.0 ** 12
W0_SCALE = 2.0 ** -4
W1_SCALE = 2.0 ** -9
OUT_SCALE = 8.0 / (X2_SCALE * W0_SCALE * W1_SCALE)


def spread_to(n):
    return sum(i not in DIRECT for i in range(n % (2 * GB), n + 1, 2 * GB))


def masked_to(n):
    return sum(i not in DIRECT for i in range(n + 1))


def ffn_of_slot(n):
    f, r = divmod(n - FFN_LAG, FG)
    early, late = (([(f - 1, 3)], [(f, 0), (f, 1)]), ([(f - 1, LAST)], [(f, 2)]))[r]
    return tuple([(i, m) for i, m in part if 0 <= i < NF] for part in (early, late))


SUMS = [at for n in range(SLOTS) for part in ffn_of_slot(n) for at in part]
HIDDEN_SUMS = [at for at in SUMS if at[1] < LAST]


def sums_to(f, m):
    return SUMS.index((f, m)) + 1


def hidden_to(f, m):
    return HIDDEN_SUMS.index((f, m)) + 1


def xattn_ffn(nc, x, ctx_in, igate_w, igate_b, fgate_w, fgate_b, ln_scale, k0, k1, k2, s0, s1, s2, running_max, out):
    with ExitStack() as stack:
        def sb(name, shape, dt=F32):
            return stack.enter_context(nc.sbuf_tensor(name, shape, dt))

        def ps(name, shape, dt=F32):
            return stack.enter_context(nc.psum_tensor(name, shape, dt))

        def sem(name):
            return stack.enter_context(nc.semaphore(name))

        ident = sb("ident", [128, 128])
        ident16 = sb("ident16", [128, 128], F16)
        gate_rows = sb("gate_rows", [2 * NH, 3 * D])
        wq = sb("wq", [128, 2, VW])
        wkv = sb("wkv", [128, 2, VW])
        bias_in = sb("bias_in", [NH, 2])
        gate_b = sb("gate_b", [128, 2])
        lns = sb("lns", [128, D])
        above = sb("above", [128, S])
        minus_half = sb("minus_half", [128, 1])
        s_in = sb("s_in", [128, 3])
        s_work = sb("s_work", [128, 8])
        k0_in = sb("k0_in", [128, 2, F], U8)
        k1_in = sb("k1_in", [128, FT, F], U8)
        k2_in = sb("k2_in", [128, FT, D], U8)
        w0 = sb("w0", [128, F], F16)
        w1 = sb("w1", [128, FT, F], F16)
        w2 = sb("w2", [128, FT, D], F16)
        xs = sb("xs", [128, B, D])
        cs_in = sb("cs_in", [128, B, D])
        vals = sb("vals", [128, 2, GB, NH, VW])
        xn = sb("xn", [128, 2 * GB, D])
        st_q = sb("st_q", [128, GB, 6])
        mv_q = sb("mv_q", [128, GB, 2])
        ve_q = sb("ve_q", [128, GB])
        rs_q = sb("rs_q", [128, GB])
        qcT = sb("qcT", [128, 2, GB, 2, S])
        q_heads = sb("q_heads", [128, 2, GB, NH, S])
        f_min = sb("f_min", [128, S])
        f_abs = sb("f_abs", [128, S])
        f_exp = sb("f_exp", [128, S])
        f_ln = sb("f_ln", [128, S])
        cumf = sb("cumf", [128, S])
        a_row = sb("a_row", [128, S])
        max_row = sb("max_row", [128, 2, S])
        m_row = sb("m_row", [128, S])
        aT = sb("aT", [128, 2, GB, VW])
        em = sb("em", [128, 2, GB, VW])
        maxb = sb("maxb", [128, 2, GB, NH, S])
        dmat = sb("dmat", [128, 2, NH, S])
        cmat = sb("cmat", [128, 2, NH, S])
        oT = sb("oT", [128, 2, 2, S])
        den = sb("den", [128, 2, NH])
        hatt = sb("hatt", [128, 2, D])
        st_h = sb("st_h", [128, 2, 6])
        mv_h = sb("mv_h", [128, 2, 2])
        ve_h = sb("ve_h", [128, 2])
        rs_h = sb("rs_h", [128, 2])
        hsc = sb("hsc", [128, 2, D])
        x1 = sb("x1", [128, XR, D])
        st_x = sb("st_x", [128, 2, 6])
        mv_x = sb("mv_x", [128, 2, 2])
        ve_x = sb("ve_x", [128, 2])
        rs_x = sb("rs_x", [128, 2])
        x2 = sb("x2", [128, 2, D])
        x2p = sb("x2p", [128, 2, 2, D], F16)
        x2T = sb("x2T", [128, 2, 2, TOK], F16)
        h1 = sb("h1", [128, FT, 2, TOK], F16)
        h2 = sb("h2", [128, FT, 2, TOK], F16)
        outb = sb("outb", [128, 2, FG, D])
        pG = ps("pG", [128, 4, S])
        pS = ps("pS", [128, NH, S])
        pO = ps("pO", [128, 4, S])
        pX = ps("pX", [128, 2, 2, TOK], F16)
        pF = [ps(f"pF{i}", [128, 2, TOK], F32) for i in range(FB)]

        ctx_loaded = [sem(f"ctx_loaded{g}") for g in range(NG)]
        x_loaded = [sem(f"x_loaded{g}") for g in range(NG)]
        gatew_loaded = sem("gatew_loaded")
        ffnw_loaded = sem("ffnw_loaded")
        ffns_loaded = sem("ffns_loaded")
        lns_loaded = sem("lns_loaded")
        ident_ready = sem("ident_ready")
        consts_ready = sem("consts_ready")
        q_heads_cleared = sem("q_heads_cleared")
        cleared = sem("cleared")
        gatew_turned = sem("gatew_turned")
        gatew_ready = sem("gatew_ready")
        ffns_ready = sem("ffns_ready")
        w02_ready = sem("w02_ready")
        w1_ready = sem("w1_ready")
        q_stats = sem("q_stats")
        q_rstd = sem("q_rstd")
        xn_ready = sem("xn_ready")
        vals_ready = sem("vals_ready")
        turned = sem("turned")
        turned_out = sem("turned_out")
        gates_ready = sem("gates_ready")
        f_min_ready = sem("f_min_ready")
        f_ln_ready = sem("f_ln_ready")
        max_ready = sem("max_ready")
        m_ready = sem("m_ready")
        am_turned = sem("am_turned")
        am_ready = sem("am_ready")
        max_stored = sem("max_stored")
        max_spread = [[sem(f"max_spread{p}{j}") for j in range(GB)] for p in range(2)]
        heads_spread = [sem(f"heads_spread{p}") for p in range(2)]
        scores_ready = sem("scores_ready")
        exp_ready = sem("exp_ready")
        direct_spread = sem("direct_spread")
        direct_masked = sem("direct_masked")
        masked = sem("masked")
        c_ready = sem("c_ready")
        pv_ready = sem("pv_ready")
        oT_ready = sem("oT_ready")
        o_turned = sem("o_turned")
        o_read = sem("o_read")
        h_stats = sem("h_stats")
        h_centre = sem("h_centre")
        h_rstd = sem("h_rstd")
        x_stats = sem("x_stats")
        x_rstd = sem("x_rstd")
        x1_ready = sem("x1_ready")
        x2_ready = sem("x2_ready")
        x2_high = sem("x2_high")
        x2_low = sem("x2_low")
        x2_turned = sem("x2_turned")
        x2T_ready = sem("x2T_ready")
        ffn_sums = sem("ffn_sums")
        ffn_high = sem("ffn_high")
        ffn_low = sem("ffn_low")
        out_ready = sem("out_ready")
        out_stored = [sem(f"out_stored{p}") for p in range(2)]
        dve_own = sem("dve_own")
        act_own = sem("act_own")
        pool_own = sem("pool_own")

        def group_rows(dram, g):
            return dram[GB * g:GB * (g + 1)].rearrange("b s d -> s b d")

        def ffn_place(f, m):
            return pF[SUMS.index((f, m)) % FB][:, :]

        def direct_place(i, half):
            if i == 1:
                return pS[:, 4 * half:4 * half + 4]
            return pF[half][:, :].rearrange("p a (h s) -> p (a h) s", s=S)

        def hidden(f, m, part):
            tile = FU * m % FT
            return (h1 if m < LAST // 2 else h2)[:, tile:tile + FU, part]

        def store(sp, f):
            sp.wait_ge(out_ready, f + 1)
            sp.dma_start(out[FG * f:FG * (f + 1)].rearrange("b s d -> s b d"),
                         outb[:, f % 2]).then_inc(out_stored[f % 2], 16)

        block = stack.enter_context(nc.Block())

        @block.sync
        def _(sp):
            def load_x(g):
                sp.dma_start(xs[:, GB * g:GB * (g + 1)], group_rows(x, g)).then_inc(x_loaded[g], 16)

            def load_ctx(g):
                sp.dma_start(cs_in[:, GB * g:GB * (g + 1)], group_rows(ctx_in, g)).then_inc(ctx_loaded[g], 16)

            load_x(0)
            for n, bias in enumerate((igate_b, fgate_b)):
                sp.dma_start(bias_in[:, n:n + 1], bias.rearrange("(h a) -> h a", a=1)).then_inc(gatew_loaded, 16)
            load_x(1)
            load_ctx(1)
            for k_dram, k_in in ((k0, k0_in), (k1, k1_in), (k2, k2_in)):
                sp.dma_start(k_in[:, :, :], k_dram.rearrange("(c p) n -> p c n", p=128)).then_inc(ffnw_loaded, 16)
            load_x(2)
            load_x(3)

            def spread_heads(g):
                sp.wait_ge(q_heads_cleared, g % 2 + 1)
                if g >= 2:
                    sp.wait_ge(scores_ready, 2 * GB * (g - 1))
                sp.wait_ge(turned_out, 2 * (g + 1))
                for h in range(NH):
                    sp.dma_start(q_heads[DH * h:DH * (h + 1), g % 2, :, h],
                                  qcT[DH * h:DH * (h + 1), g % 2, :, 0]).then_inc(heads_spread[g % 2], 16)

            for g in range(NG):
                spread_heads(g)
                p = g % 2
                sp.wait_ge(max_ready, g + 1)
                sp.dma_start(running_max[g], max_row[:, p, :]).then_inc(max_stored, 16)
                sp.wait_ge(max_stored, 16 * (g + 1))
                if g >= 2:
                    sp.wait_ge(exp_ready, GB * (g - 1))
                for j in range(GB):
                    if GB * g + j not in DIRECT:
                        sp.dma_start(maxb[:, p, j], running_max[g:g + 1, 32 * j:32 * j + NH].broadcast_to(
                            [128, NH, S])).then_inc(max_spread[p][j], 16)
                if g == 0:
                    load_ctx(2)
                    load_ctx(3)
            for f in range(NF):
                store(sp, f)
            for p in range(2):
                sp.wait_ge(out_stored[p], 16 * (NF // 2))

        @block.tensor
        def _(pe):
            def turn(g, part):
                if part == 1:
                    pe.wait_ge(ctx_loaded[g], 16)
                    if g >= 1:
                        pe.wait_ge(am_ready, g)
                else:
                    pe.wait_ge(xn_ready, GB * (g + 1))
                    pe.wait_ge(turned_out, 2 * g + 1)
                for n in range(GB * g, GB * (g + 1)):
                    last = pe.transpose(pG[:, n % GB], cs_in[:, n] if part == 1 else xn[:, n % (2 * GB)], ident[:, :])
                last.then_inc(turned, 1)

            def gates(g):
                if g == 0:
                    pe.wait_ge(gatew_ready, 1)
                pe.wait_ge(turned_out, 2 * (g + 1))
                for n in range(2):
                    for part, w in enumerate((wq, wkv)):
                        for j in range(GB):
                            last = pe.matmul(pG[32 * j:32 * j + VW, n], w[:, n, :], qcT[:, g % 2, j, part],
                                             start=(part == 0), stop=(part == 1))
                last.then_inc(gates_ready, 1)

            def turn_am(g):
                pe.wait_ge(m_ready, g + 1)
                pe.transpose(pG[:, 2], a_row[:, :], ident[:, :])
                pe.transpose(pG[:, 3], m_row[:, :], ident[:, :]).then_inc(am_turned, 1)

            def spread_max(i):
                g, j = divmod(DIRECT[i], GB)
                pe.wait_ge(max_ready, g + 1)
                for h in range(NH):
                    row = 32 * j + h
                    last = pe.matmul(direct_place(i, h // 4)[:, h % 4], ident[:, row:row + 1].broadcast_to([128, 128]),
                                     max_row[:, g % 2], start=True, stop=True)
                last.then_inc(direct_spread, 1)

            def scores(n):
                g, j = divmod(n, GB)
                if j == 0:
                    pe.wait_ge(heads_spread[g % 2], 16 * NH * (g // 2 + 1))
                if n == 0:
                    pe.wait_ge(direct_masked, 2)
                for half in range(2):
                    if n >= 1:
                        pe.wait_ge(c_ready, 2 * (n - 1) + half + 1)
                    pe.matmul(pS[:, 4 * half:4 * half + 4].rearrange("p h s -> p (h s)"), qcT[:, g % 2, j, 1],
                              q_heads[:, g % 2, j, 4 * half:4 * half + 4].rearrange("p h s -> p (h s)"),
                              start=True, stop=True).then_inc(scores_ready, 1)

            def weigh(n):
                pe.wait_ge(vals_ready, n + 1)
                if n >= 1:
                    pe.wait_ge(o_read, n)
                for half in range(2):
                    pe.wait_ge(c_ready, 2 * n + half + 1)
                    for i in range(4):
                        h = 4 * half + i
                        last = pe.matmul(pO[32 * i:32 * i + VW, half], vals[:, n // GB % 2, n % GB, h],
                                         cmat[:, n % 2, h], start=True, stop=True)
                last.then_inc(pv_ready, 1)

            def turn_o(n):
                pe.wait_ge(oT_ready, n + 1)
                for half in range(2):
                    last = pe.transpose(pO[:, 2 + half], oT[:, n % 2, half], ident[:, :])
                last.then_inc(o_turned, 1)

            def turn_x2(n):
                f, j = divmod(n, FG)
                if j == 0 and f >= 2:
                    pe.wait_ge(x2T_ready, f - 1)
                pe.wait_ge(x2_high, n + 1)
                pe.wait_ge(x2_low, n + 1)
                for part in range(2):
                    last = pe.transpose(pX[:, f % 2, part, S * j:S * (j + 1)], x2p[:, n % 2, part], ident16[:, :])
                last.then_inc(x2_turned, 1)

            def ffn(f, m):
                at = SUMS.index((f, m))
                if at >= FB:
                    f_before, m_before = SUMS[at - FB]
                    if m_before == LAST:
                        pe.wait_ge(out_ready, f_before + 1)
                    else:
                        pe.wait_ge(ffn_low, hidden_to(f_before, m_before))
                bank = ffn_place(f, m)
                if m == LAST:
                    for j in range(FG):
                        for k in range(FT):
                            if j == 0 and k % FU == 0:
                                pe.wait_ge(ffn_low, hidden_to(f, LAST // 2 + k // FU))
                            for part in range(2):
                                last = pe.matmul(bank[:, 0, D * j:D * (j + 1)], h2[:, k, part, S * j:S * (j + 1)],
                                                 w2[:, k], start=(k == 0 and part == 0),
                                                 stop=(k == FT - 1 and part == 1))
                    last.then_inc(ffn_sums, 1)
                    return
                for u in range(FU):
                    tile = (FU * m + u) % FT
                    columns = slice(128 * tile, 128 * (tile + 1))
                    if m < LAST // 2:
                        if m == 0:
                            pe.wait_ge(w02_ready, 1)
                            pe.wait_ge(x2T_ready, f + 1)
                        for part in range(2):
                            last = pe.matmul(bank[:, u], w0[:, columns], x2T[:, f % 2, part],
                                             start=(part == 0), stop=(part == 1))
                    else:
                        pe.wait_ge(w1_ready, 1)
                        for k in range(FT):
                            if u == 0 and k % FU == 0:
                                pe.wait_ge(ffn_low, hidden_to(f, k // FU))
                            for part in range(2):
                                last = pe.matmul(bank[:, u], w1[:, k, columns], h1[:, k, part],
                                                 start=(k == 0 and part == 0), stop=(k == FT - 1 and part == 1))
                last.then_inc(ffn_sums, 1)

            def keep_busy(products):
                for _ in range(products):
                    pe.matmul(pF[FB - 1][:, 0, 0:128], ident[:, :], ident[:, :], start=True, stop=True)

            pe.wait_ge(ident_ready, 1)
            keep_busy(8)
            pe.wait_ge(consts_ready, 1)
            pe.wait_ge(gatew_loaded, 16 * 4)
            for part in range(3):
                last = pe.transpose(pF[0][0:D, 0, 2 * NH * part:2 * NH * (part + 1)], gate_rows[:, D * part:D * (part + 1)],
                                    ident[0:2 * NH, 0:2 * NH])
            for j in range(GB):
                last = pe.matmul(pF[0][32 * j:32 * j + VW, 0, 6 * NH:6 * NH + 2], ident[0:NH, 0:VW], bias_in[:, :], start=True, stop=True)
            last.then_inc(gatew_turned, 1)
            turn(0, 1)
            keep_busy(2)
            turn(0, 0)
            keep_busy(2)
            gates(0)
            keep_busy(10)
            spread_max(0)
            turn_am(0)
            spread_max(1)
            turn(1, 1)
            turn(1, 0)
            scores(0)
            gates(1)
            for n in range(SLOTS):
                g, k = divmod(n, GB)
                prepare = n < B and g + 1 < NG
                early, late = ffn_of_slot(n)
                if prepare and k == 0 and n > 0:
                    gates(g + 1)
                if 0 < n < B:
                    scores(n)
                if prepare and (k == 1 and g > 0 or n == 2):
                    turn_am(g + 1)
                if k == 3 and g + 2 < NG:
                    turn(g + 2, 1)
                if 0 <= n - 1 < B:
                    weigh(n - 1)
                if 0 <= n - 4 < B:
                    turn_x2(n - 4)
                if k == 3 and g + 2 < NG:
                    turn(g + 2, 0)
                for f, m in early:
                    ffn(f, m)
                if 0 <= n - 1 < B:
                    turn_o(n - 1)
                for f, m in late:
                    ffn(f, m)

        @block.scalar
        def _(act):
            own = [0]

            def step(ins):
                own[0] += 1
                ins.then_inc(act_own, 1)
                act.wait_ge(act_own, own[0])

            def turn_out(g, part):
                act.wait_ge(turned, 2 * g + 2 - part)
                if part == 1 and g >= 2:
                    act.wait_ge(scores_ready, 2 * GB * (g - 1))
                act.copy(qcT[:, g % 2, :, part], pG[:, :]).then_inc(turned_out, 1)

            def gate_logs(g):
                act.wait_ge(f_min_ready, g + 1)
                step(act.activation(f_abs[:, :], pG[:, 1], ACT.Abs, bias=gate_b[:, 1:2]))
                step(act.activation(f_exp[:, :], f_abs[:, :], ACT.Exp, scale=-1.0))
                act.activation(f_ln[:, :], f_exp[:, :], ACT.Ln, bias=1.0).then_inc(f_ln_ready, 1)

            def ffn_weights_1():
                act.wait_ge(ffns_ready, 1)
                act.wait_ge(ffnw_loaded, 16 * 3)
                act.activation(w1[:, :, :], k1_in[:, :, :], ACT.Identity, bias=s_work[:, 6:7],
                               scale=s_work[:, 5:6]).then_inc(w1_ready, 1)

            def gate_out(g):
                act.wait_ge(am_turned, g + 1)
                if g >= 2:
                    act.wait_ge(o_read, GB * (g - 1))
                act.copy(aT[:, g % 2].rearrange("p j h -> p (j h)"), pG[:, 2])
                e = em[:, g % 2].rearrange("p j h -> p (j h)")
                step(act.activation(e, pG[:, 3], ACT.Exp, scale=-1.0))
                act.activation(e, e, ACT.Copy, bias=EPS).then_inc(am_ready, 1)

            def decay(n, heads):
                if n >= B:
                    return
                g, j = divmod(n, GB)
                if heads[0] == 0:
                    act.wait_ge(am_ready, g + 1)
                    if n in DIRECT:
                        act.wait_ge(direct_masked, DIRECT.index(n) + 1)
                    else:
                        act.wait_ge(masked, masked_to(n))
                    if n >= 2:
                        act.wait_ge(c_ready, 2 * (n - 1))
                for h in heads:
                    last = act.activation(dmat[:, n % 2, h], maxb[:, g % 2, j, h], ACT.Exp,
                                          bias=aT[:, g % 2, j, h:h + 1], scale=-1.0)
                if heads[-1] == NH - 1:
                    last.then_inc(exp_ready, 1)

            def take_o(n):
                act.wait_ge(pv_ready, n + 1)
                if n >= 2:
                    act.wait_ge(o_turned, n - 1)
                act.copy(oT[:, n % 2], pO[:, 0:2]).then_inc(oT_ready, 1)

            def x2_take_high(n):
                act.wait_ge(x2_ready, n + 1)
                if n >= 2:
                    act.wait_ge(x2_turned, n - 1)
                act.copy(x2p[:, n % 2, 0], x2[:, n % 2]).then_inc(x2_high, 1)

            def high(f, m):
                if m == LAST:
                    return
                act.wait_ge(ffn_sums, sums_to(f, m))
                act.activation(hidden(f, m, 0), ffn_place(f, m), ACT.Relu).then_inc(ffn_high, 1)

            act.preload_act_table_set("natural_log_exp_and_others")
            act.dma_start(cs_in[:, 0:GB], group_rows(ctx_in, 0)).then_inc(ctx_loaded[0], 16)
            act.dma_start(gate_rows[0:NH, :], igate_w).then_inc(gatew_loaded, 16)
            act.dma_start(gate_rows[NH:2 * NH, :], fgate_w).then_inc(gatew_loaded, 16)
            act.dma_start(lns[:, :], ln_scale.rearrange("(a d) -> a d", a=1).broadcast_to([128, D])).then_inc(lns_loaded, 16)
            for i, s in enumerate((s0, s1, s2)):
                act.dma_start(s_in[:, i:i + 1], s.rearrange("(a d) -> a d", a=1).broadcast_to([128, 1])).then_inc(ffns_loaded, 16)
            act.wait_ge(consts_ready, 1)
            turn_out(0, 1)
            turn_out(0, 0)
            gate_logs(0)
            ffn_weights_1()
            gate_out(0)
            decay(0, range(NH // 2))
            turn_out(1, 1)
            decay(0, range(NH // 2, NH))
            turn_out(1, 0)
            for n in range(SLOTS):
                g, k = divmod(n, GB)
                prepare = n < B and g + 1 < NG
                for f, m in ffn_of_slot(n - 1)[1]:
                    high(f, m)
                if prepare and k == 0 and n > 0:
                    gate_logs(g + 1)
                if prepare and k == 1 and g > 0:
                    gate_out(g + 1)
                if n == 1:
                    take_o(0)
                if k == 3 and g + 2 < NG:
                    turn_out(g + 2, 1)
                if 1 <= n - 1 < B:
                    take_o(n - 1)
                if k == 3 and g + 2 < NG:
                    turn_out(g + 2, 0)
                if n == 2:
                    gate_out(1)
                decay(n + 1, range(NH))
                for f, m in ffn_of_slot(n)[0]:
                    high(f, m)
                if 0 <= n - 3 < B:
                    x2_take_high(n - 3)
                if n == 0:
                    gate_logs(1)

        @block.vector
        def _(dve):
            own = [0]

            def mark(ins):
                own[0] += 1
                ins.then_inc(dve_own, 1)
                return own[0]

            def step(ins):
                dve.wait_ge(dve_own, mark(ins))

            def q_statistics(n):
                if n >= B:
                    return None
                if n % GB == 0:
                    dve.wait_ge(x_loaded[n // GB], 16)
                return mark(dve.bn_stats(st_q[:, n % GB], xs[:, n]))

            def q_moments(n, stats):
                if n >= B:
                    return
                dve.wait_ge(dve_own, stats)
                if n >= GB:
                    dve.wait_ge(q_rstd, n - GB + 1)
                dve.bn_aggr(mv_q[:, n % GB], st_q[:, n % GB]).then_inc(q_stats, 1)

            def norm_q(n):
                if n >= B:
                    return
                dve.wait_ge(q_rstd, n + 1)
                dve.wait_ge(q_stats, n + 1)
                if n >= 2 * GB and n % GB == 0:
                    dve.wait_ge(turned, 2 * (n // GB - 1))
                dve.tensor_scalar(xn[:, n % (2 * GB)], xs[:, n], mv_q[:, n % GB, 0:1], rs_q[:, n % GB:n % GB + 1],
                                  ALU.subtract, ALU.mult).then_inc(xn_ready, 1)

            def forget_min(g):
                dve.wait_ge(gates_ready, g + 1)
                dve.tensor_scalar(f_min[:, :], pG[:, 1], gate_b[:, 1:2], 0.0, ALU.add, ALU.min).then_inc(f_min_ready, 1)

            def gate_scans(g):
                dve.wait_ge(f_ln_ready, g + 1)
                dve.wait_ge(f_min_ready, g + 1)
                step(dve.tensor_tensor_scan(cumf[:, :], f_min[:, :], f_ln[:, :], 0.0, ALU.add, ALU.subtract))
                if g >= 1:
                    dve.wait_ge(am_turned, g)
                step(dve.scalar_tensor_tensor(out=a_row[:, :], in0=pG[:, 0], scalar=gate_b[:, 0:1], in1=cumf[:, :],
                                              op0=ALU.add, op1=ALU.subtract))
                if g >= 2:
                    dve.wait_ge(max_stored, 16 * (g - 1))
                dve.tensor_tensor_scan(max_row[:, g % 2], a_row[:, :], a_row[:, :], LOWEST,
                                       ALU.max, ALU.max).then_inc(max_ready, 1)
                dve.wait_ge(max_ready, g + 1)
                dve.tensor_tensor(m_row[:, :], cumf[:, :], max_row[:, g % 2], ALU.add).then_inc(m_ready, 1)

            def direct_mask(i):
                g, j = divmod(DIRECT[i], GB)
                dve.wait_ge(direct_spread, i + 1)
                dve.wait_ge(consts_ready, 1)
                for half in range(2):
                    last = dve.tensor_tensor(maxb[:, g % 2, j, 4 * half:4 * half + 4], direct_place(i, half),
                                             above[:, :].unsqueeze(1).broadcast_to([128, 4, S]), ALU.max)
                last.then_inc(direct_masked, 1)

            def make_c(n):
                dve.wait_ge(exp_ready, n + 1)
                if n >= 2:
                    dve.wait_ge(pv_ready, n - 1)
                for half in range(2):
                    part = slice(4 * half, 4 * half + 4)
                    dve.wait_ge(scores_ready, 2 * n + half + 1)
                    dve.scalar_tensor_tensor(out=cmat[:, n % 2, part].rearrange("p h s -> p (h s)"),
                                             in0=pS[:, part].rearrange("p h s -> p (h s)"), scalar=QK_SCALE,
                                             in1=dmat[:, n % 2, part].rearrange("p h s -> p (h s)"),
                                             op0=ALU.mult, op1=ALU.mult).then_inc(c_ready, 1)

            def by_head(n):
                return pO[:, 2:4].rearrange("p a (i v) -> p (a i) v", v=VW)

            def normalizer_1(n):
                dve.wait_ge(o_turned, n + 1)
                dve.wait_ge(am_ready, n // GB + 1)
                return mark(dve.scalar_tensor_tensor(out=den[:, n % 2], in0=by_head(n)[:, :, ONE], scalar=EPS,
                                                     in1=em[:, n // GB % 2, n % GB, 0:NH],
                                                     op0=ALU.subtract, op1=ALU.max, reverse0=True))

            def normalizer_2(n, before):
                dve.wait_ge(dve_own, before)
                return mark(dve.scalar_tensor_tensor(out=den[:, n % 2], in0=by_head(n)[:, :, ONE], scalar=EPS,
                                                     in1=den[:, n % 2], op0=ALU.add, op1=ALU.max))

            def normalizer_3(n, before):
                dve.wait_ge(dve_own, before)
                return mark(dve.reciprocal(den[:, n % 2], den[:, n % 2]))

            def head_out(n, before):
                dve.wait_ge(dve_own, before)
                dve.tensor_tensor(hatt[:, n % 2].rearrange("p (h d) -> p h d", d=DH), by_head(n)[:, :, 0:DH],
                                  den[:, n % 2].unsqueeze(2).broadcast_to([128, NH, DH]), ALU.mult).then_inc(o_read, 1)

            def h_statistics(n):
                dve.wait_ge(o_read, n + 1)
                return mark(dve.bn_stats(st_h[:, n % 2], hatt[:, n % 2]))

            def h_moments(n, before):
                dve.wait_ge(dve_own, before)
                dve.bn_aggr(mv_h[:, n % 2], st_h[:, n % 2]).then_inc(h_stats, 1)

            def h_centred(n):
                if n == 0:
                    dve.wait_ge(lns_loaded, 16)
                dve.wait_ge(h_stats, n + 1)
                dve.scalar_tensor_tensor(out=hsc[:, n % 2], in0=hatt[:, n % 2], scalar=mv_h[:, n % 2, 0:1],
                                         in1=lns[:, :], op0=ALU.subtract, op1=ALU.mult).then_inc(h_centre, 1)

            def residual(n):
                if not 0 <= n < B:
                    return
                if n >= XR and n % FG == 0:
                    dve.wait_ge(out_ready, (n - XR) // FG + 1)
                dve.wait_ge(h_centre, n + 1)
                dve.wait_ge(h_rstd, n + 1)
                dve.scalar_tensor_tensor(out=x1[:, n % XR], in0=hsc[:, n % 2], scalar=rs_h[:, n % 2:n % 2 + 1],
                                         in1=xs[:, n], op0=ALU.mult, op1=ALU.add).then_inc(x1_ready, 1)

            def x_statistics(n):
                dve.wait_ge(x1_ready, n + 1)
                return mark(dve.bn_stats(st_x[:, n % 2], x1[:, n % XR]))

            def x_moments(n, before):
                dve.wait_ge(dve_own, before)
                dve.bn_aggr(mv_x[:, n % 2], st_x[:, n % 2]).then_inc(x_stats, 1)

            def norm_x(n):
                if not 0 <= n < B:
                    return
                e = n % 2
                dve.wait_ge(x_rstd, n + 1)
                dve.wait_ge(x_stats, n + 1)
                if n >= 2:
                    dve.wait_ge(x2_low, n - 1)
                dve.tensor_scalar(x2[:, e], x1[:, n % XR], mv_x[:, e, 0:1], rs_x[:, e:e + 1],
                                  ALU.subtract, ALU.mult).then_inc(x2_ready, 1)

            def take_x2T(f):
                dve.wait_ge(x2_turned, FG * (f + 1))
                if f >= 2:
                    dve.wait_ge(ffn_sums, sums_to(f - 2, LAST // 2 - 1))
                dve.tensor_copy(x2T[:, f % 2], pX[:, f % 2]).then_inc(x2T_ready, 1)

            def low(f, m):
                if m == LAST:
                    dve.wait_ge(ffn_sums, sums_to(f, m))
                    if f >= 2:
                        dve.wait_ge(out_stored[f % 2], 16 * (f // 2))
                    dve.scalar_tensor_tensor(out=outb[:, f % 2].rearrange("p j d -> p (j d)"), in0=ffn_place(f, m)[:, 0],
                                             scalar=s_work[:, 7:8],
                                             in1=x1[:, FG * f % XR:FG * f % XR + FG].rearrange("p j d -> p (j d)"),
                                             op0=ALU.mult, op1=ALU.add).then_inc(out_ready, 1)
                    return
                dve.wait_ge(ffn_high, hidden_to(f, m))
                dve.scalar_tensor_tensor(out=hidden(f, m, 1), in0=ffn_place(f, m), scalar=0.0, in1=hidden(f, m, 0),
                                         op0=ALU.max, op1=ALU.subtract).then_inc(ffn_low, 1)

            def ffn_scalars():
                dve.wait_ge(ffns_loaded, 16 * 3)
                step(dve.tensor_scalar(s_work[:, 0:2], s_in[:, 0:2], 0.0, 2.0, ALU.is_ge, ALU.mult))
                step(dve.tensor_scalar(s_work[:, 0:2], s_work[:, 0:2], 1.0, None, ALU.subtract))
                step(dve.tensor_tensor(s_work[:, 2:4], s_work[:, 0:2], s_in[:, 0:2], ALU.mult))
                step(dve.tensor_scalar(s_work[:, 4:5], s_work[:, 0:1], W0_SCALE, None, ALU.mult))
                step(dve.tensor_scalar(s_work[:, 5:6], s_work[:, 1:2], 2.0 * W1_SCALE, None, ALU.mult))
                step(dve.tensor_scalar(s_work[:, 6:7], s_work[:, 1:2], -W1_SCALE, None, ALU.mult))
                step(dve.tensor_tensor(s_work[:, 7:8], s_work[:, 2:3], s_work[:, 3:4], ALU.mult))
                step(dve.tensor_tensor(s_work[:, 7:8], s_work[:, 7:8], s_in[:, 2:3], ALU.mult))
                dve.tensor_scalar(s_work[:, 7:8], s_work[:, 7:8], OUT_SCALE, None, ALU.mult).then_inc(ffns_ready, 1)

            def ffn_weights_0_2():
                dve.wait_ge(ffns_ready, 1)
                dve.wait_ge(ffnw_loaded, 16 * 3)
                step(dve.tensor_tensor(w0[:, :], k0_in[:, 0], k0_in[:, 1], ALU.subtract))
                step(dve.tensor_scalar(w0[:, :], w0[:, :], s_work[:, 4:5], None, ALU.mult))
                dve.tensor_scalar(w2[:, :, :], k2_in[:, :, :], 2.0, 1.0, ALU.mult, ALU.subtract).then_inc(w02_ready, 1)

            def gate_cols(part):
                return pF[0][0:D, 0, 2 * NH * part:2 * NH * (part + 1)].rearrange("p (n h) -> p n h", n=2)

            step(dve.memset(wq[:, :, :], 0.0))
            dve.memset(wkv[:, :, :], 0.0).then_inc(cleared, 1)
            dve.wait_ge(cleared, 1)
            def q_group(g):
                at = q_statistics(GB * g)
                for n in range(GB * g, GB * (g + 1)):
                    after = q_statistics(n + 1) if n + 1 < GB * (g + 1) else None
                    q_moments(n, at)
                    at = after

            def norm_group(g):
                for n in range(GB * g, GB * (g + 1)):
                    norm_q(n)

            q_group(0)
            norm_group(0)
            dve.wait_ge(gatew_turned, 1)
            step(dve.tensor_copy(gate_b[:, :], pF[0][:, 0, 6 * NH:6 * NH + 2]))
            step(dve.tensor_copy(wq[:, :, 0:NH], gate_cols(0)))
            step(dve.tensor_copy(wkv[:, :, 0:NH], gate_cols(1)))
            dve.tensor_tensor(wkv[:, :, 0:NH], gate_cols(2), wkv[:, :, 0:NH], ALU.add).then_inc(gatew_ready, 1)
            q_group(1)
            ffn_scalars()
            forget_min(0)
            norm_group(1)
            gate_scans(0)
            q_group(2)
            direct_mask(0)
            direct_mask(1)
            ffn_weights_0_2()
            for n in range(SLOTS):
                g, k = divmod(n, GB)
                prepare = n < B and g + 1 < NG
                before = ffn_of_slot(n - 1)[1]
                early, late = ffn_of_slot(n)
                behind = 0 <= n - 1 < B
                for f, m in before:
                    low(f, m)
                if prepare and k == 0 and n > 0:
                    forget_min(g + 1)
                if n < B:
                    make_c(n)
                if n == 0:
                    forget_min(1)
                    norm_group(2)
                    gate_scans(1)
                if prepare and k == 0 and n > 0:
                    gate_scans(g + 1)
                if (n - FFN_LAG) % FG == 0 and 0 <= n - FFN_LAG < B:
                    take_x2T((n - FFN_LAG) // FG)
                q_at = q_statistics(n + 3 * GB)
                if behind:
                    at = normalizer_1(n - 1)
                if n >= 1:
                    norm_q(n + 3 * GB - 1)
                if behind:
                    at = normalizer_2(n - 1, at)
                residual(n - 2)
                if behind:
                    at = normalizer_3(n - 1, at)
                norm_x(n - 3)
                if behind:
                    head_out(n - 1, at)
                if 0 <= n - 2 < B:
                    x_at = x_statistics(n - 2)
                if behind:
                    at = h_statistics(n - 1)
                q_moments(n + 3 * GB, q_at)
                if 0 <= n - 2 < B:
                    x_moments(n - 2, x_at)
                if behind:
                    h_moments(n - 1, at)
                for f, m in early:
                    low(f, m)
                if behind:
                    h_centred(n - 1)

        @block.gpsimd
        def _(pool):
            own = [0]

            def step(ins):
                own[0] += 1
                ins.then_inc(pool_own, 1)
                pool.wait_ge(pool_own, own[0])

            def rstd(dst, var, work, scale):
                step(pool.tensor_scalar(work, var, LN_EPS, scale, ALU.add, ALU.mult))
                return pool.tensor_tensor(dst, work, minus_half[:, :], ALU.pow)

            def q_scale(n, count=1):
                if n >= B:
                    return
                e = n % GB
                pool.wait_ge(q_stats, n + count)
                if n >= GB:
                    pool.wait_ge(xn_ready, n + count - GB)
                step(pool.tensor_scalar(ve_q[:, e:e + count], mv_q[:, e:e + count, 1], LN_EPS, None, ALU.add))
                pool.tensor_tensor(rs_q[:, e:e + count], ve_q[:, e:e + count],
                                   minus_half[:, :].broadcast_to([128, count]), ALU.pow).then_inc(q_rstd, count)

            def take_values(n):
                if n >= B:
                    return
                g, j = divmod(n, GB)
                if j == 0:
                    pool.wait_ge(ctx_loaded[g], 16)
                if n >= 2 * GB:
                    pool.wait_ge(pv_ready, n - 2 * GB + 1)
                pool.tensor_copy(vals[:, g % 2, j, :, 0:DH], cs_in[:, n].rearrange("p (h d) -> p h d", d=DH)).then_inc(vals_ready, 1)

            def mask(n):
                if n >= B:
                    return
                g, j = divmod(n, GB)
                if n in DIRECT:
                    return
                pool.wait_ge(max_spread[g % 2][j], 16 * spread_to(n))
                pool.affine_select(out=maxb[:, g % 2, j], in_=maxb[:, g % 2, j], compare_op=ALU.is_ge, fill=NEVER,
                                   base=0, pattern=[[0, NH], [1, S]], channel_multiplier=-1).then_inc(masked, 1)

            def h_scale(n):
                e = n % 2
                pool.wait_ge(h_stats, n + 1)
                if n >= 2:
                    pool.wait_ge(x1_ready, n - 1)
                rstd(rs_h[:, e:e + 1], mv_h[:, e, 1:2], ve_h[:, e:e + 1], 1.0).then_inc(h_rstd, 1)

            def x_scale(n):
                e = n % 2
                pool.wait_ge(x_stats, n + 1)
                if n >= 2:
                    pool.wait_ge(x2_ready, n - 1)
                rstd(rs_x[:, e:e + 1], mv_x[:, e, 1:2], ve_x[:, e:e + 1], X2_SCALE ** -2).then_inc(x_rstd, 1)

            def x2_take_low(n):
                pool.wait_ge(x2_high, n + 1)
                pool.tensor_tensor(x2p[:, n % 2, 1], x2[:, n % 2], x2p[:, n % 2, 0], ALU.subtract).then_inc(x2_low, 1)

            step(pool.memset(minus_half[:, :], -0.5))
            step(pool.memset(ident[:, :], 0.0))
            pool.affine_select(out=ident[:, :], in_=ident[:, :], compare_op=ALU.not_equal, fill=1.0, base=0,
                               pattern=[[-1, 128]], channel_multiplier=1).then_inc(ident_ready, 1)
            pool.wait_ge(ident_ready, 1)
            step(pool.tensor_copy(ident16[:, :], ident[:, :]))
            step(pool.memset(above[:, :], NEVER))
            step(pool.affine_select(out=above[:, :], in_=above[:, :], compare_op=ALU.is_gt, fill=LOWEST,
                                    base=0, pattern=[[-1, S]], channel_multiplier=1))
            step(pool.memset(vals[:, :, :, :, DH:VW], 0.0))
            pool.memset(vals[:, :, :, :, ONE:ONE + 1], 1.0).then_inc(consts_ready, 1)
            pool.wait_ge(consts_ready, 1)
            q_scale(0, GB)
            pool.memset(q_heads[:, 0], 0.0).then_inc(q_heads_cleared, 1)
            q_scale(GB, GB)
            pool.memset(q_heads[:, 1], 0.0).then_inc(q_heads_cleared, 1)
            take_values(0)
            take_values(1)
            q_scale(2 * GB, GB)
            for n in range(SLOTS):
                mask(n + 2)
                if n < 2:
                    take_values(n + 2)
                take_values(n + GB)
                if 0 <= n - 3 < B:
                    x2_take_low(n - 3)
                q_scale(n + 3 * GB)
                if 0 <= n - 2 < B:
                    x_scale(n - 2)
                if 0 <= n - 1 < B:
                    h_scale(n - 1)


_INS = ['x', 'ctx_1024', 'L0_xattn_igate_w', 'L0_xattn_igate_b', 'L0_xattn_fgate_w', 'L0_xattn_fgate_b',
        'L0_xattn_ln_scale', 'L0_ffn_k0', 'L0_ffn_k1', 'L0_ffn_k2', 'L0_ffn_s0', 'L0_ffn_s1', 'L0_ffn_s2']


def kernel(**inputs):
    import numpy as np
    import concourse.bacc as bacc
    from concourse.bass_utils import run_bass_kernel_spmd

    nc = bacc.Bacc("TRN2", target_bir_lowering=False, num_devices=1)
    arrays, args = {}, []
    for name in _INS:
        a = np.ascontiguousarray(inputs[name])
        arrays[f"in_{name}"] = a
        args.append(nc.dram_tensor(f"in_{name}", a.shape, mybir.dt.from_np(a.dtype), kind="ExternalInput").ap())
    running_max = nc.dram_tensor("running_max", [NG, 128, S], F32, kind="Internal").ap()
    out = nc.dram_tensor("out", [B, S, D], F32, kind="ExternalOutput").ap()
    xattn_ffn(nc, *args, running_max, out)
    result = run_bass_kernel_spmd(nc, [arrays], core_ids=[0])
    return result.results[0]["out"]
```
